# Optimizing a Trainium2 kernel written in Bass

```python
import numpy as np
import jax
import jax.numpy as jnp

def _softmax(x, axis=-1):
    return jax.nn.softmax(x, axis=axis)

def _gelu(x):
    return jax.nn.gelu(x, approximate=True)

def _silu(x):
    return jax.nn.silu(x)

def _sigmoid(x):
    return jax.nn.sigmoid(x)

def _layernorm(x, axis=-1, eps=1e-05):
    m = jnp.mean(x, axis=axis, keepdims=True)
    v = jnp.var(x, axis=axis, keepdims=True)
    return (x - m) / jnp.sqrt(v + eps)

def _scatter_add(tgt, idx, src, axis=0):
    return tgt.at[idx].add(src)

def _segment_sum(src, seg, n):
    return jax.ops.segment_sum(src, seg, n)
kernel_name = 'mk_adj_resnorm_d4_adj_r2_d961c8'

def setup_inputs(seed: int=0):
    np.random.seed(seed)
    _w = jnp.asarray

    def _rec_inputs():
        import jax
        import jax.numpy as jnp
        _gk = jax.random.key(seed)
        x = -0.001547 + 1.001 * jax.random.normal(jax.random.fold_in(_gk, 1), (8192, 64), jnp.float32)
        _w = (1.0 + jnp.arange(8192, dtype=jnp.float32)) ** (-0.5)
        _w = _w / _w.mean()
        _pij = jnp.clip(0.000976562 * _w[:, None] * _w[None, :], 0.0, 1.0)
        _a = jax.random.uniform(jax.random.fold_in(_gk, 2), (8192, 8192)) < _pij
        _a = jnp.logical_or(_a, jnp.eye(8192, dtype=bool))
        _af = _a.astype(jnp.float32)
        adj = _af
        return (x, adj)
    x, adj = _rec_inputs()

    def _L0_gnn_setup():
        import jax, jax.numpy as jnp
        import numpy as np
        N = 2048
        F = 64
        H = 8
        D = 8
        key = jax.random.key(seed)
        k1, k2, k3, k4, k5, k6 = jax.random.split(key, 6)
        X = jax.random.normal(k1, (N, F), dtype=jnp.float32)
        A = (jax.random.uniform(k2, (N, N)) < 0.01).astype(jnp.float32)
        A = jnp.maximum(A, jnp.eye(N, dtype=jnp.float32))
        lim_w = np.sqrt(6.0 / (F + H * D)).astype(np.float32)
        W = jax.random.uniform(k3, (F, H * D), minval=-lim_w, maxval=lim_w, dtype=jnp.float32)
        lim_a = np.sqrt(6.0 / (1 + H * D)).astype(np.float32)
        att_self = jax.random.uniform(k4, (H, D), minval=-lim_a, maxval=lim_a, dtype=jnp.float32)
        att_neigh = jax.random.uniform(k5, (H, D), minval=-lim_a, maxval=lim_a, dtype=jnp.float32)
        bias = jnp.zeros((H, D), dtype=jnp.float32)
        return {'X': X, 'A': A, 'W': W, 'att_self': att_self, 'att_neigh': att_neigh, 'bias': bias}
    _L0_gnn_all = _L0_gnn_setup()
    _L0_gnn_in = {k: v for k, v in _L0_gnn_all.items() if k in ('W', 'att_self', 'att_neigh', 'bias')}
    del _L0_gnn_all

    def _L1_gnn_setup():
        import jax, jax.numpy as jnp
        import numpy as np
        N = 5000
        DIM = 64
        F_CONST = 1.0
        B_CONST = 0.1
        R_CONST = 0.01
        key = jax.random.key(seed)
        k1, k2 = jax.random.split(key)
        t = jnp.zeros((1,), dtype=jnp.float32)
        x = jax.random.uniform(k1, (N, DIM), dtype=jnp.float32)
        A = jax.random.uniform(k2, (N, N), dtype=jnp.float32)
        return {'t': t, 'x': x, 'A': A}
    _L1_gnn_all = _L1_gnn_setup()
    _L1_gnn_in = {k: v for k, v in _L1_gnn_all.items() if k in ('t',)}
    del _L1_gnn_all

    def _L2_gnn_setup():
        import jax, jax.numpy as jnp
        import numpy as np
        N, D = (6144, 64)

        def _ggc(x, adj, W, wih, whh, bih, bhh):
            m = adj @ (x @ W)
            gi = m @ wih.T + bih
            gh = x @ whh.T + bhh
            i_r, i_z, i_n = jnp.split(gi, 3, axis=-1)
            h_r, h_z, h_n = jnp.split(gh, 3, axis=-1)
            r = jax.nn.sigmoid(i_r + h_r)
            z = jax.nn.sigmoid(i_z + h_z)
            n = jnp.tanh(i_n + r * h_n)
            return (1.0 - z) * n + z * x
        key = jax.random.key(seed)
        ks = jax.random.split(key, 8)
        s = 1.0 / np.sqrt(D)
        return {'x': jax.random.normal(ks[0], (N, D), jnp.float32), 'adj': jax.random.uniform(ks[1], (N, N), jnp.float32), 'W1': jax.random.normal(ks[2], (D, D), jnp.float32) * s, 'wih1': jax.random.normal(ks[3], (3 * D, D), jnp.float32) * s, 'whh1': jax.random.normal(ks[4], (3 * D, D), jnp.float32) * s, 'bih1': jnp.zeros((3 * D,), jnp.float32), 'bhh1': jnp.zeros((3 * D,), jnp.float32), 'W2': jax.random.normal(ks[5], (D, D), jnp.float32) * s, 'wih2': jax.random.normal(ks[6], (3 * D, D), jnp.float32) * s, 'whh2': jax.random.normal(ks[7], (3 * D, D), jnp.float32) * s, 'bih2': jnp.zeros((3 * D,), jnp.float32), 'bhh2': jnp.zeros((3 * D,), jnp.float32)}
    _L2_gnn_all = _L2_gnn_setup()
    _L2_gnn_in = {k: v for k, v in _L2_gnn_all.items() if k in ('W1', 'wih1', 'whh1', 'bih1', 'bhh1', 'W2', 'wih2', 'whh2', 'bih2', 'bhh2')}
    del _L2_gnn_all

    def _L3_gnn_setup():
        import jax, jax.numpy as jnp
        import numpy as np
        N = 8192
        F = 64
        O = 64
        key = jax.random.key(seed)
        k1, k2, k3 = jax.random.split(key, 3)
        features = jax.random.normal(k1, (N, F), dtype=jnp.float32)
        adj = jax.random.uniform(k2, (N, N), dtype=jnp.float32)
        W = jax.random.normal(k3, (O, 2 * F), dtype=jnp.float32)
        return {'features': features, 'adj': adj, 'W': W}
    _L3_gnn_all = _L3_gnn_setup()
    _L3_gnn_in = {k: v for k, v in _L3_gnn_all.items() if k in ('W',)}
    del _L3_gnn_all
    return {'x': x, 'adj': adj, 'L0_gnn_W': _L0_gnn_in['W'], 'L0_gnn_att_self': _L0_gnn_in['att_self'], 'L0_gnn_att_neigh': _L0_gnn_in['att_neigh'], 'L0_gnn_bias': _L0_gnn_in['bias'], 'L1_gnn_t': _L1_gnn_in['t'], 'L2_gnn_W1': _L2_gnn_in['W1'], 'L2_gnn_wih1': _L2_gnn_in['wih1'], 'L2_gnn_whh1': _L2_gnn_in['whh1'], 'L2_gnn_bih1': _L2_gnn_in['bih1'], 'L2_gnn_bhh1': _L2_gnn_in['bhh1'], 'L2_gnn_W2': _L2_gnn_in['W2'], 'L2_gnn_wih2': _L2_gnn_in['wih2'], 'L2_gnn_whh2': _L2_gnn_in['whh2'], 'L2_gnn_bih2': _L2_gnn_in['bih2'], 'L2_gnn_bhh2': _L2_gnn_in['bhh2'], 'L3_gnn_W': _L3_gnn_in['W']}

def reference(x, adj, L0_gnn_W, L0_gnn_att_self, L0_gnn_att_neigh, L0_gnn_bias, L1_gnn_t, L2_gnn_W1, L2_gnn_wih1, L2_gnn_whh1, L2_gnn_bih1, L2_gnn_bhh1, L2_gnn_W2, L2_gnn_wih2, L2_gnn_whh2, L2_gnn_bih2, L2_gnn_bhh2, L3_gnn_W):
    import jax
    import jax.numpy as jnp

    def _L0_gnn_ref(X, A, W, att_self, att_neigh, bias):
        import jax, jax.numpy as jnp
        import numpy as np
        N = 2048
        F = 64
        H = 8
        D = 8
        feats = (X @ W).reshape(-1, H, D)
        a_self = jnp.einsum('nhd,hd->nh', feats, att_self)
        a_neigh = jnp.einsum('nhd,hd->nh', feats, att_neigh)
        scores = a_self.T[:, :, None] + a_neigh.T[:, None, :]
        scores = jax.nn.leaky_relu(scores, negative_slope=0.2)
        scores = scores + (-10000000000.0 * (1.0 - A))[None, :, :]
        attn = jax.nn.softmax(scores, axis=-1)
        out = jnp.einsum('hij,jhd->ihd', attn, feats)
        out = out + bias[None, :, :]
        out = out.reshape(-1, H * D)
        return jax.nn.relu(out)

    def _L1_gnn_ref(t, x, A):
        import jax, jax.numpy as jnp
        import numpy as np
        N = 5000
        DIM = 64
        F_CONST = 1.0
        B_CONST = 0.1
        R_CONST = 0.01
        Ax = A @ x
        outer = R_CONST * jnp.sum(x * Ax, axis=1, keepdims=True)
        return F_CONST - B_CONST * x - outer

    def _L2_gnn_ref(x, adj, W1, wih1, whh1, bih1, bhh1, W2, wih2, whh2, bih2, bhh2):
        import jax, jax.numpy as jnp
        import numpy as np
        N, D = (6144, 64)

        def _ggc(x, adj, W, wih, whh, bih, bhh):
            m = adj @ (x @ W)
            gi = m @ wih.T + bih
            gh = x @ whh.T + bhh
            i_r, i_z, i_n = jnp.split(gi, 3, axis=-1)
            h_r, h_z, h_n = jnp.split(gh, 3, axis=-1)
            r = jax.nn.sigmoid(i_r + h_r)
            z = jax.nn.sigmoid(i_z + h_z)
            n = jnp.tanh(i_n + r * h_n)
            return (1.0 - z) * n + z * x
        h = jax.nn.relu(_ggc(x, adj, W1, wih1, whh1, bih1, bhh1))
        return jax.nn.relu(_ggc(h, adj, W2, wih2, whh2, bih2, bhh2))

    def _L3_gnn_ref(features, adj, W):
        import jax, jax.numpy as jnp
        import numpy as np
        N = 8192
        F = 64
        O = 64
        deg = jnp.sum(adj, axis=1, keepdims=True)
        neigh = adj @ features / (deg + 1.0)
        data = jnp.concatenate([features, neigh], axis=-1)
        return data @ W.T
    x = _layernorm(x + _L0_gnn_ref(x, adj, L0_gnn_W, L0_gnn_att_self, L0_gnn_att_neigh, L0_gnn_bias), axis=-1)
    x = _layernorm(x + _L1_gnn_ref(L1_gnn_t, x, adj), axis=-1)
    x = _layernorm(x + _L2_gnn_ref(x, adj, L2_gnn_W1, L2_gnn_wih1, L2_gnn_whh1, L2_gnn_bih1, L2_gnn_bhh1, L2_gnn_W2, L2_gnn_wih2, L2_gnn_whh2, L2_gnn_bih2, L2_gnn_bhh2), axis=-1)
    x = _layernorm(x + _L3_gnn_ref(x, adj, L3_gnn_W), axis=-1)
    return x

_drawn_inputs = setup_inputs


def setup_inputs(seed=0):
    import zlib

    import numpy as np

    out = dict(_drawn_inputs(seed))
    spreads = {'L0_gnn_bias': (0.0, 0.1),
     'L2_gnn_bih1': (0.0, 0.462),
     'L2_gnn_bhh1': (0.0, 0.586),
     'L2_gnn_bih2': (0.0, 0.421),
     'L2_gnn_bhh2': (0.0, 0.554)}
    factors = {}
    for name, (base, spread) in spreads.items():
        noise = np.random.default_rng([zlib.crc32(name.encode()), seed]).standard_normal(out[name].shape)
        drawn = base * np.exp(spread * noise) if base else spread * noise
        out[name] = jnp.asarray(drawn.astype(out[name].dtype))
    for name, factor in factors.items():
        out[name] = (out[name] * factor).astype(out[name].dtype)
    return out
```

```python
from contextlib import ExitStack

import concourse.bass as bass
from concourse import mybir

F32, BF16, F16 = mybir.dt.float32, mybir.dt.bfloat16, mybir.dt.float16
F8, U8, U16, I32, U32 = (mybir.dt.float8e4, mybir.dt.uint8, mybir.dt.uint16, mybir.dt.int32,
                         mybir.dt.uint32)
ALU = mybir.AluOpType
ACT = mybir.ActivationFunctionType
AX = mybir.AxisListType

P = 128
N, D, H = 8192, 64, 8
DH = D // H
T = N // P
CH, HALF = 1024, 512
NC = N // CH
NH = N // HALF
BT = 8
NB = T // BT
CT = CH // P
HT = HALF // P
NG, GH = 2, 4
IT = NC * NG
VC = DH + 1
SPLIT = 3
HW = 64
AVC = SPLIT * GH * VC + 1
AVP = 112
WC = AVP + GH * HW
RING = 6
WSLOTS = 4
CREDIT = 32
BIG = float(2 ** 40)
ONE8 = 56.0
VS = 4096.0
EPS = 1e-5
QT = T // 4
GATES = 256
BANKS = 6


def dve_heads(jt):
    return [0] if jt % 4 == 3 else [0, 1]


K_BLOCK, K_POST, K_FIRST = 5, 6, 26
K_PASS = {1: 27, 2: 8, 3: 28, 4: 21}


V_CMP = sum(len(dve_heads(j)) for j in range(T))
S_CMP = GH * T - V_CMP


class Count:

    def __init__(self, base):
        self.base, self.n = base, 0

    def up(self):
        self.n += 1
        return 1

    def now(self):
        return self.base + self.n


def build(nc, adj, xT, xN, W0, attS, attN, bias0, W1T, wihT, whhT, bih, bhh, W3T, consts, out):
    with ExitStack() as ctx:
        def sb(name, shape, dt):
            return ctx.enter_context(nc.sbuf_tensor(name, shape, dt))

        def sem(name):
            return ctx.enter_context(nc.semaphore(name))

        adj8 = nc.dram_tensor("adj8", (NH, 4, P, 2, BT * HALF), U8, kind="Internal").ap()
        w_tab = nc.dram_tensor("w_tab", (NG, NB, P, BT * WC), BF16, kind="Internal").ap()
        s_rows = nc.dram_tensor("s_rows", (NC, H, CH), F32, kind="Internal").ap()

        abuf = sb("abuf", [P, NB, 2, BT, HALF], U8)
        a8 = abuf[:].bitcast(F8)
        a16 = abuf[:].bitcast(U16)
        wring = sb("wring", [P, WSLOTS, BT, WC], BF16)
        early = sb("early", [P, GH * CH * 4 + RING * GH * CH], U8)
        srow = early[:, 0:GH * CH * 4].bitcast(F32).rearrange("p (h r) -> p h r", h=GH)
        masks = early[:, GH * CH * 4:].rearrange("p (s h f k) -> p s h f k", s=RING, h=GH, f=2)
        masks8 = masks.bitcast(F8)
        masks16 = masks.bitcast(U16)
        VB = T * P * 2
        vals = [early[:, i * VB:(i + 1) * VB].bitcast(F16).rearrange("p (f m k) -> p f m k", f=NH, m=HT)
                for i in range(2)]
        stage_at = GH * CH * 4
        WST = NG * BT * WC * 2
        wst = [early[:, stage_at + i * WST:stage_at + (i + 1) * WST].bitcast(BF16)
               .rearrange("p (g t w) -> p g t w", g=NG, t=BT) for i in range(2)]
        gbuf = sb("gbuf", [P, BANKS * HALF * 4], U8)
        drained = gbuf[:].bitcast(F32).rearrange("p (b k) -> p b k", b=BANKS)
        v18 = gbuf[:, 0:BT * H * 2 * VC * 4].bitcast(F32).rearrange("p (t h k) -> p t h k", t=BT, h=H)
        ybuf = [drained[:, i, :] for i in range(2)]
        xt_sb = drained[:, 2, :]
        gates = gbuf[:, 3 * 2048:5 * 2048].bitcast(F32).rearrange("p (m k) -> p m k", m=HT)
        xbuf = sb("xbuf", [P, T * D], F32)
        x_hf = xbuf[:].rearrange("p (f m d) -> p f m d", f=NH, m=HT)
        s_self = xbuf[:, 0:512].rearrange("p (t h) -> p t h", t=T)
        s_neigh = xbuf[:, 512:1024].rearrange("p (t h) -> p t h", t=T)
        dd = xbuf[:, 1024:1536].rearrange("p (t h) -> p t h", t=T)
        e1 = xbuf[:, 1536:2048].rearrange("p (t h) -> p t h", t=T)
        e2 = xbuf[:, 2048:2560].rearrange("p (t h) -> p t h", t=T)
        obuf = sb("obuf", [P, T * D], F32)
        feats = obuf[:].rearrange("p (t h d) -> p t h d", t=T, h=H)
        o_it = obuf[:].rearrange("p (i m k) -> p i m k", i=IT, m=CT)
        h_hf = obuf[:].rearrange("p (f m d) -> p f m d", f=NH, m=HT)
        xT_sb = abuf[0:D, NB // 2:, :, :, :].rearrange("p a b c d -> p (a b c d)").bitcast(F32)
        srowT = gbuf[:, 9216:9216 + 2048].bitcast(F32).rearrange("p (q k) -> p q k", q=4)
        bn = sb("bn", [P, IT, CT, GH], F32)
        nthr = sb("nthr", [P, NG, T, GH], F32)
        nbig = sb("nbig", [P, NG, T, GH], F32)
        thr = sb("thr", [P, T, GH], F32)
        stepbias = sb("stepbias", [P, T, GH], F32)
        rdeg = sb("rdeg", [P, IT, CT], F32)
        t1 = sb("t1", [P, CT, GH, VC], F32)
        rden = sb("rden", [P, CT, GH], F32)
        u = sb("u", [P, HT, D], F32)
        q = sb("q", [P, HT, D], F32)
        nn = sb("nn", [P, HT, D], F32)
        hh = sb("hh", [P, HT, D], F32)
        st = sb("st", [P, 8, HT], F32)
        obs = sb("obs", [P, 2, HT, D], F32)
        w0 = sb("w0", [D, D], F32)
        att = sb("att", [D, 2, D], F32)
        watt = sb("watt", [D, 16], F32)
        wtmp = sb("wtmp", [D, 2, D], F32)
        b0 = sb("b0", [P, D], F32)
        selP = sb("selP", [P, 2 * 2 * VC], F32)
        selA = sb("selA", [P, GH * VC + 1], F32)
        sel2 = sb("sel2", [P, D], F32)
        identf = sb("identf", [P, P], F32)
        ident = sb("ident", [P, P], F16)
        nmax = sb("nmax", [P, H], F32)
        nall = sb("nall", [P, H], F32)
        w1t = sb("w1t", [D, 2, 2, D], F32)
        wih = sb("wih", [D, 2, 3 * D], F32)
        rx = sb("rx", [P, 2, 3 * D], F32)
        ry = sb("ry", [P, 2, 3 * D], F32)
        gb = sb("gb", [P, 2, GATES], F32)
        gb2 = sb("gb2", [P, 2, 2 * D], F32)
        wa = sb("wa", [P, D], F32)
        wb = sb("wb", [P, D], F32)

        ps = ctx.enter_context(nc.psum_tensor("ps", [P, 8, HALF], F32))
        z0 = ps[:, 6:8, :].rearrange("p b (m k) -> p (b m) k", m=4)
        zz = [ps[:, 4 + 2 * i:6 + 2 * i, :].rearrange("p b (m k) -> p (b m) k", m=2) for i in range(2)]

        params = sem("params")
        xT_in = sem("xT_in")
        x_in = sem("x_in")
        watt_ready = sem("watt_ready")
        nat_ready = sem("nat_ready")
        ns_ready = sem("ns_ready")
        turned = sem("turned")
        turned_out = sem("turned_out")
        rows_stored = sem("rows_stored")
        feats_ready = sem("feats_ready")
        feats_out = sem("feats_out")
        nmax_ready = sem("nmax_ready")
        nall_ready = sem("nall_ready")
        dd_ready = sem("dd_ready")
        exps_ready = sem("exps_ready")
        relu_ready = sem("relu_ready")
        bn_ready = sem("bn_ready")
        zeroed = sem("zeroed")
        cast_done = sem("cast_done")
        rest_ready = sem("rest_ready")
        packed = sem("packed")
        w_stored = [sem(f"w_stored{i}") for i in range(2)]
        dve_step = sem("dve_step")
        a_loaded = [sem(f"a_loaded{b}") for b in range(NB)]
        a_stored = [sem(f"a_stored{b}") for b in range(NB)]
        w_loaded = [sem(f"w_loaded{k}") for k in range(WSLOTS)]
        s_loaded = [sem(f"s_loaded{h}") for h in range(GH)]
        cmp_v = sem("cmp_v")
        cmp_s = sem("cmp_s")
        thr_ready = sem("thr_ready")
        stepbias_ready = sem("stepbias_ready")
        masked = sem("masked")
        tiles_done = sem("tiles_done")
        drained_v = sem("drained_v")
        drained_s = sem("drained_s")
        z_ready = sem("z_ready")
        z_used = sem("z_used")
        gate = sem("gate")
        ry_ready = sem("ry_ready")
        consts_ready = sem("consts_ready")
        v_ready = sem("v_ready")
        q_loaded = [sem(f"q_loaded{k}") for k in range(8)]
        q_done = sem("q_done")
        y_out = sem("y_out")
        xt_ready = sem("xt_ready")
        xt_out = sem("xt_out")
        xz_done = sem("xz_done")
        zz_ready = sem("zz_ready")
        zz_used = sem("zz_used")
        gates_out = sem("gates_out")
        cand_in = sem("cand_in")
        cand_out = sem("cand_out")
        row_out = sem("row_out")
        stored = sem("stored")

        block = ctx.enter_context(nc.Block())

        def lead(eng):
            eng.sem_inc(gate, 1)

        def chunk_of(it):
            return it // NG

        n_small = 8 + 2 * (1 + 4 + 4) + 4

        @block.sync
        def _(sp):
            def small(dst, src):
                sp.dma_start(dst, src).then_inc(params, 16)

            small(w0[:], W0)
            small(att[:, 0, :], attS.partition_broadcast(D))
            small(att[:, 1, :], attN.partition_broadcast(D))
            sp.dma_start(xT_sb, xT).then_inc(xT_in, 16)
            small(b0[:], bias0.partition_broadcast(P))
            small(identf[:], consts[:, 0:P])
            small(selP[:], consts[:, P:P + 36])
            small(selA[:], consts[:, P + 36:P + 73])
            small(sel2[:], consts[:, P + 73:P + 73 + D])
            for k in range(2):
                small(wih[:, k, :], wihT[k])
                for r in range(2):
                    small(w1t[:, k, r, :], W1T[k])
                    small(rx[r * D:(r + 1) * D, k, :], whhT[k])
                small(gb[:, k, 0:2 * D], bih[k, 0:2 * D].partition_broadcast(P))
                small(gb2[:, k, :], bhh[k, 0:2 * D].partition_broadcast(P))
                small(gb[:, k, 2 * D:3 * D], bhh[k, 2 * D:3 * D].partition_broadcast(P))
                small(gb[:, k, 3 * D:4 * D], bih[k, 2 * D:3 * D].partition_broadcast(P))
            for r in range(2):
                small(wa[r * D:(r + 1) * D, :], W3T[0:D, :])
                small(wb[r * D:(r + 1) * D, :], W3T[D:2 * D, :])
            for k in range(4):
                sp.wait_ge(turned_out, k + 1)
                lead(sp)
                for c in range(2):
                    sp.dma_start(s_rows[2 * k + c].rearrange("h (m p) -> m h p", p=P),
                                 srowT[c * D:(c + 1) * D, k, :]).then_inc(rows_stored, 16)
            with sp.Fori(0, NB // 2) as k:
                for i in range(2):
                    sp.wait_ge(cast_done, k * 12 + (i * 6 + 12))
                    lead(sp)
                    sp.wait_ge(packed, k * 12 + (i * 6 + 6))
                    lead(sp)
                    sp.dma_start(w_tab[:, k * 2 + i, :, :].rearrange("g p w -> p g w"),
                                 wst[i].rearrange("p g t w -> p g (t w)")).then_inc(w_stored[i], 16)
            for i in range(2):
                sp.wait_ge(w_stored[i], 16 + 8 * NB)
            sp.wait_ge(rows_stored, 16 * 8)
            sp.wait_ge(rest_ready, 3 * NB)
            sp.wait_ge(relu_ready, 1)
            sp.dma_start(xbuf[:], xN).then_inc(x_in, 16)
            with sp.Fori(0, NC) as c:
                for g in range(NG):
                    for b in range(NB):
                        sp.wait_ge(tiles_done,
                                   c * (NG * T) + (g * T + CREDIT + (b - WSLOTS + 1) * BT))
                        lead(sp)
                        sp.dma_start(wring[:, b % WSLOTS, :, :].rearrange("p t w -> p (t w)"),
                                     w_tab[g, b, :, :]).then_inc(w_loaded[b % WSLOTS], 16)
                        if b == 2:
                            sp.wait_ge(cmp_v, c * (NG * V_CMP) + (g * V_CMP + 1))
                            lead(sp)
                            sp.wait_ge(cmp_s, c * (NG * S_CMP) + (g * S_CMP + 1))
                            lead(sp)
                            for h in range(GH):
                                sp.dma_start(srow[:, h, :],
                                             s_rows[c, g * GH + h, :].partition_broadcast(P)
                                             ).then_inc(s_loaded[h], 16)
                        if g == 0:
                            sp.wait_ge(a_loaded[b], c * 16 + 16)
                            lead(sp)
                            sp.dma_start(
                                adj8[bass.ds(c * 2, 2), b // 2, :, b % 2, :].rearrange("f p k -> p f k"),
                                abuf[:, b, :, :, :].rearrange("p f t k -> p f (t k)")
                            ).then_inc(a_stored[b], 16)
            for b in range(NB):
                sp.wait_ge(a_stored[b], 16 * NC)
            sp.wait_ge(tiles_done, CREDIT + IT * T)
            for p in range(4):
                with sp.Fori(0, NC) as c:
                    for slot in range(8):
                        sp.wait_ge(q_done, c * 8 + (p * 64 + slot + 1))
                        lead(sp)
                        sp.dma_start(abuf[:, slot, :, :, :].rearrange("p f t k -> p (f t k)"),
                                     adj8[c * 2 + slot // 4, slot % 4, :, :, :].rearrange("p b k -> p (b k)")
                                     ).then_inc(q_loaded[slot], 16)
            with sp.Fori(0, NH) as n:
                sp.wait_ge(row_out, n + 2)
                lead(sp)
                sp.dma_start(out[:, n, :], h_hf[:, n, :, :].rearrange("p m d -> p (m d)")
                             ).then_inc(stored, 16)
            sp.wait_ge(stored, 16 * NH)

        @block.gpsimd
        def _(pool):
            def load_adj(c, b):
                pool.dma_start(a8[:, b, :, :, :].rearrange("p f t k -> p (f t k)"),
                               adj[c, b, :, :]).then_inc(a_loaded[b], 16)

            for i in range(2):
                pool.memset(wst[i].rearrange("p g t w -> p (g t w)").bitcast(U32), 0).then_inc(zeroed, 1)
            pool.wait_ge(zeroed, 2)
            for i in range(2):
                pool.memset(wst[i][:, :, :, AVC - 1:AVC], 1.0).then_inc(zeroed, 1)
            for b in range(NB // 2):
                load_adj(0, b)
            pool.wait_ge(nmax_ready, 1)
            pool.partition_all_reduce(nall[:], nmax[:], P, bass.bass_isa.ReduceOp.max).then_inc(nall_ready, 1)
            with pool.Fori(0, NB // 2) as k:
                for i in range(2):
                    for s in range(SPLIT):
                        for g in range(NG):
                            pool.wait_ge(cast_done, k * 12 + (i * 6 + s * 2 + g + 7))
                            lead(pool)
                            pool.tensor_copy(
                                wst[i][:, g, :, s * GH * VC:(s + 1) * GH * VC].rearrange(
                                    "p t (h k) -> p t h k", h=GH),
                                wst[i][:, g, :, AVP:].rearrange("p t (h w) -> p t h w", h=GH)[
                                    :, :, :, s * 2 * VC + VC:(s + 1) * 2 * VC]).then_inc(packed, 1)
            pool.wait_ge(feats_ready, NB)
            for b in range(NB // 2, NB):
                load_adj(0, b)
            for c in range(1, NC):
                for b in range(NB):
                    pool.wait_ge(tiles_done, CREDIT + (2 * c - 1) * T + (b + 1) * BT)
                    pool.wait_ge(a_stored[b], 16 * c)
                    load_adj(c, b)

        @block.tensor
        def _(pe):
            pe.sem_inc(tiles_done, CREDIT)
            pe.sem_inc(z_ready, 1)
            pe.sem_inc(q_done, 8)
            pe.wait_ge(xT_in, 16)
            pe.wait_ge(watt_ready, 2)
            nat = ps[:, 0:2, :].rearrange("p b (t k) -> p (b t) k", k=16)
            for k in range(T // 8):
                for m in range(8):
                    mm = pe.matmul(nat[:, k * 8 + m, :], xT_sb[:, (k * 8 + m) * P:(k * 8 + m + 1) * P],
                                   watt[:], start=True, stop=True)
                mm.then_inc(nat_ready, 1)
            for k in range(NB):
                pe.wait_ge(feats_out, k + 1)
                for m in range(8):
                    mm = pe.matmul(ps[:, 6 + k % 2, m * D:(m + 1) * D],
                                   xT_sb[:, (k * 8 + m) * P:(k * 8 + m + 1) * P], w0[:],
                                   start=True, stop=True)
                mm.then_inc(feats_ready, 1)
            pe.wait_ge(ns_ready, 2)
            pe.wait_ge(params, 16 * n_small)
            for k in range(4):
                pe.matmul(ps[:, 2 + k, 0:P], xbuf[:, k * P:(k + 1) * P], identf[:],
                          start=True, stop=True).then_inc(turned, 1)
            for k in range(2):
                mm = pe.matmul(ps[:, 0, k * 192:(k + 1) * 192], w1t[:, k, :, :].rearrange("p r d -> p (r d)"),
                               wih[:, k, :], start=True, stop=True)
            mm.then_inc(ry_ready, 1)
            pe.wait_ge(turned_out, 4)
            pe.wait_ge(feats_out, 2 + NB)
            pe.wait_ge(consts_ready, 1)

            def tile_sums(it, b, t):
                jt = b * BT + t
                ws = wring[:, b % WSLOTS, t, :]
                if t == 0:
                    pe.wait_ge(w_loaded[b % WSLOTS], it * 32 + (16 * (b // WSLOTS) + 16))
                    lead(pe)
                pe.wait_ge(masked, it * T + (jt + 1))
                lead(pe)
                for f in range(2):
                    for h in range(GH):
                        r = (h % 2) * HW
                        pe.matmul(ps[r:r + HW, f * 3 + h // 2, :], ws[:, AVP + h * HW:AVP + (h + 1) * HW],
                                  masks8[:, jt % RING, h, f, :], start=(jt == 0), stop=(jt == T - 1),
                                  skip_group_check=True)
                    mm = pe.matmul(ps[0:AVC, f * 3 + 2, :], ws[:, 0:AVC], a8[:, b, f, t, :],
                                   start=(jt == 0), stop=(jt == T - 1))
                mm.then_inc(tiles_done, 1)

            def gather(it):
                pe.wait_ge(drained_v, it * 3 + 6)
                pe.wait_ge(drained_s, it * 3 + 6)
                pe.wait_ge(z_used, it + 1)
                lead(pe)
                for f in range(2):
                    for m in range(HT):
                        for k in range(3):
                            rows = AVC if k == 2 else P
                            w = GH * VC + 1 if k == 2 else 4 * VC
                            mm = pe.matmul(z0[:, f * HT + m, k * 36:k * 36 + w],
                                           drained[0:rows, f * 3 + k, m * P:(m + 1) * P],
                                           (selA if k == 2 else selP)[0:rows, :], start=True, stop=True)
                mm.then_inc(z_ready, 1)

            def attention_step(it, behind):
                pe.wait_ge(drained_v, it * 3 + 3)
                pe.wait_ge(drained_s, it * 3 + 3)
                lead(pe)
                for b in range(NB):
                    for t in range(BT):
                        tile_sums(it, b, t)
                        if behind and b == 0 and t == 3:
                            gather(it - 1)

            attention_step(0, False)
            with pe.Fori(1, IT) as it:
                attention_step(it, True)
            gather(IT - 1)
            pe.wait_ge(consts_ready, 8)
            pe.wait_ge(z_used, IT + 1)

            def x_part(p, n, f):
                pe.wait_ge(xt_out, n - (NH - 1))
                pe.wait_ge(zz_used, n)
                lead(pe)
                w, cols = (rx[:, p - 2, :], 3 * D) if p < 4 else (wa[:], D)
                for m in range(HT):
                    mm = pe.matmul(zz[f][:, m, 0:cols], xt_sb[:, m * P:(m + 1) * P], w,
                                   start=(m % 2 == 0), stop=True, skip_group_check=True)
                mm.then_inc(xz_done, 1)

            def y_part(p, n, f, first=False):
                pe.wait_ge(y_out, n + 1)
                if p == 1 and not first:
                    pe.wait_ge(zz_used, n)
                lead(pe)
                for m in range(HT):
                    lhs = ybuf[f][:, m * P:(m + 1) * P]
                    if p == 1:
                        mm = pe.matmul(zz[f][:, m, 0:D], lhs, sel2[:], start=(m % 2 == 0), stop=True,
                                       skip_group_check=True)
                    elif p == 4:
                        mm = pe.matmul(zz[f][:, m, D:2 * D], lhs, wb[:], start=False, stop=True,
                                       skip_group_check=True)
                    else:
                        pe.matmul(zz[f][:, m, 0:2 * D], lhs, ry[:, p - 2, 0:2 * D], start=False, stop=True,
                                  skip_group_check=True)
                        mm = pe.matmul(zz[f][:, m, 3 * D:4 * D], lhs, ry[:, p - 2, 2 * D:3 * D],
                                       start=False, stop=True, skip_group_check=True)
                mm.then_inc(zz_ready, 1)

            def pass_half(p, c, f, behind):
                base = (p - 1) * NH
                n = c * 2 + (base + f)
                first = isinstance(c, int)
                v = vals[(p - 1) % 2]
                if not (first and n < 2):
                    pe.wait_ge(y_out, n - 1)
                    lead(pe)
                for jt in range(T):
                    slot = f * 4 + jt // QT
                    if jt % QT == 0:
                        pe.wait_ge(q_loaded[slot], c * 16 + ((p - 1) * NC * 16 + 16))
                        lead(pe)
                    if first and jt % HT == 0:
                        pe.wait_ge(v_ready, base + jt // HT + 1)
                    mm = pe.matmul(ps[:, f, :], v[:, jt // HT, jt % HT, :],
                                   a8[:, slot, (jt % QT) // BT, jt % BT, :],
                                   start=(jt == 0), stop=(jt == T - 1))
                    if jt % QT == QT - 1:
                        mm.then_inc(q_done, 1)
                    if p > 1 and jt == 8:
                        if not (first and n == NH):
                            pe.wait_ge(xt_out, n - NH)
                            lead(pe)
                        for m in range(HT):
                            mm = pe.matmul(ps[:, 2, m * P:(m + 1) * P], v[:, c * 2 + f, m, :], ident[:],
                                           start=True, stop=True)
                        mm.then_inc(xt_ready, 1)
                    if behind and jt == 20:
                        y_part(p, n - 1, 1 - f, first and n == 1)
                    if p > 1 and jt == 56:
                        x_part(p, n, f)

            for p in range(1, 5):
                pass_half(p, 0, 0, False)
                pass_half(p, 0, 1, True)
                with pe.Fori(1, NC) as c:
                    pass_half(p, c, 0, True)
                    pass_half(p, c, 1, True)
                y_part(p, p * NH - 1, 1)

        @block.scalar
        def _(act):
            act.sem_inc(feats_out, 2)
            act.sem_inc(drained_s, 3)
            act.sem_inc(cmp_s, 1)
            for i in range(2):
                act.sem_inc(w_stored[i], 16)
            act.sem_inc(cast_done, 6)
            for k in range(NB):
                act.wait_ge(feats_ready, k + 1)
                act.copy(obuf[:, k * 512:(k + 1) * 512], ps[:, 6 + k % 2, :]).then_inc(feats_out, 1)
            for k in range(4):
                act.wait_ge(turned, k + 1)
                act.copy(srowT[:, k, :], ps[:, 2 + k, 0:P]).then_inc(turned_out, 1)
            act.wait_ge(dd_ready, 1)
            act.activation(e1, dd, ACT.Exp).then_inc(exps_ready, 1)
            act.activation(e2, dd, ACT.Exp, scale=0.2).then_inc(exps_ready, 1)
            act.wait_ge(relu_ready, 1)
            act.activation(bn[:], bn[:], ACT.Exp, scale=-0.8).then_inc(bn_ready, 1)
            act.wait_ge(zeroed, 4)
            with act.Fori(0, NB // 2) as k:
                for i in range(2):
                    for s in range(SPLIT):
                        act.wait_ge(rest_ready, k * 6 + (i * 3 + s + 1))
                        if s == 0:
                            act.wait_ge(w_stored[i], k * 16 + 16)
                        lead(act)
                        for g in range(NG):
                            act.copy(wst[i][:, g, :, AVP:].rearrange("p t (h w) -> p t h w", h=GH)[
                                :, :, :, s * 2 * VC:(s + 1) * 2 * VC],
                                v18[:, :, g * GH:(g + 1) * GH, :]).then_inc(cast_done, 1)
            for i in range(2):
                act.wait_ge(w_stored[i], 16 + 8 * NB)

            def attention_step(it):
                act.wait_ge(cmp_s, it * S_CMP + 1)
                lead(act)
                act.copy(stepbias[:], nbig[:, it % 2, :, :]).then_inc(stepbias_ready, 1)
                act.wait_ge(stepbias_ready, it + 1)
                lead(act)
                for jt in range(T):
                    act.wait_ge(tiles_done, it * T + (CREDIT + jt + 1 - RING))
                    lead(act)
                    for h in range(len(dve_heads(jt)), GH):
                        if jt == 0 or (h == 1 and jt == 3):
                            act.wait_ge(s_loaded[h], it * 16 + 16)
                            lead(act)
                        act.activation(masks8[:, jt % RING, h, :, :].rearrange("p f k -> p (f k)"),
                                       srow[:, h, :], ACT.Sigmoid, bias=stepbias[:, jt, h:h + 1],
                                       scale=BIG, saturate=False).then_inc(cmp_s, 1)
                act.wait_ge(tiles_done, it * T + (CREDIT + T))
                act.wait_ge(z_ready, it + 1)
                for k in (1, 3, 5):
                    rows = AVC if k % 3 == 2 else P
                    act.copy(drained[0:rows, k, :], ps[0:rows, k, :]).then_inc(drained_s, 1)

            with act.Fori(0, IT) as it:
                attention_step(it)
            act.wait_ge(z_used, IT + 1)

            def pass_half(p, c, f, first):
                n = c * 2 + ((p - 1) * NH + f)
                if p > 1:
                    act.wait_ge(xt_ready, n - (NH - 1))
                    if not (first and n == NH):
                        act.wait_ge(xz_done, n - NH)
                    act.copy(xt_sb, ps[:, 2, :]).then_inc(xt_out, 1)
                act.wait_ge(q_done, n * 4 + 12)
                if not (first and n < 2):
                    act.wait_ge(zz_ready, n - 1)
                act.copy(ybuf[f], ps[:, f, :]).then_inc(y_out, 1)
                if p in (2, 3):
                    act.wait_ge(zz_used, n + 2)
                    act.activation(gates[:, :, 0:2 * D], gates[:, :, 0:2 * D], ACT.Sigmoid
                                   ).then_inc(gates_out, 1)
                    act.wait_ge(cand_in, n - (NH - 1))
                    act.activation(nn[:], nn[:], ACT.Tanh).then_inc(cand_out, 1)

            for p in range(1, 5):
                for f in range(2):
                    pass_half(p, 0, f, True)
                with act.Fori(1, NC) as c:
                    for f in range(2):
                        pass_half(p, c, f, False)

        @block.vector
        def _(dve):
            dve.sem_inc(drained_v, 3)
            dve.sem_inc(cmp_v, 1)
            dve.sem_inc(z_used, 1)
            dve.sem_inc(zz_used, 1)
            dve.sem_inc(row_out, 1)
            k = Count(0)
            dve.wait_ge(params, 16 * n_small)
            for i in range(2):
                dve.tensor_tensor(wtmp[:, i, :], w0[:], att[:, i, :], ALU.mult).then_inc(dve_step, k.up())
            dve.wait_ge(dve_step, k.now())
            for i in range(2):
                dve.tensor_reduce(watt[:, i * H:(i + 1) * H],
                                  wtmp[:, i, :].rearrange("f (h d) -> f h d", h=H),
                                  AX.X, ALU.add).then_inc(watt_ready, 1)
            dve.wait_ge(nat_ready, T // 8)
            nat = ps[:, 0:2, :].rearrange("p b (t k) -> p (b t) k", k=16)
            dve.tensor_copy(s_self, nat[:, :, 0:H]).then_inc(ns_ready, 1)
            dve.tensor_copy(s_neigh, nat[:, :, H:2 * H]).then_inc(ns_ready, 1)
            dve.wait_ge(ns_ready, 2)
            dve.tensor_reduce(nmax[:], s_neigh.rearrange("p t h -> p h t"), AX.X, ALU.max
                              ).then_inc(nmax_ready, 1)
            for g in range(NG):
                own = s_neigh[:, :, g * GH:(g + 1) * GH]
                dve.tensor_scalar(nthr[:, g, :, :], own, -1.0, None, ALU.mult).then_inc(dve_step, k.up())
                dve.tensor_scalar(nbig[:, g, :, :], own, BIG, None, ALU.mult).then_inc(dve_step, k.up())
            dve.wait_ge(nall_ready, 1)
            dve.tensor_tensor(dd, s_neigh, nall[:].unsqueeze(1).to_broadcast([P, T, H]),
                              ALU.subtract).then_inc(dd_ready, 1)
            bn4 = bn[:].rearrange("p (c g) m h -> p c g m h", g=NG)
            ns4 = s_self.rearrange("p (c m) k -> p c m k", m=CT)
            for g in range(NG):
                hs = slice(g * GH, (g + 1) * GH)
                dve.tensor_tensor(bn4[:, :, g], ns4[:, :, :, hs],
                                  nall[:, hs].unsqueeze(1).unsqueeze(1).to_broadcast([P, NC, CT, GH]),
                                  ALU.add).then_inc(dve_step, k.up())
            dve.wait_ge(dve_step, k.now())
            dve.tensor_scalar(bn[:], bn[:], 0.0, None, ALU.max).then_inc(relu_ready, 1)
            dve.wait_ge(ry_ready, 1)
            dve.tensor_scalar(ry[:].rearrange("p k w -> p (k w)"), ps[:, 0, 0:384], 1.0 / VS, None, ALU.mult
                              ).then_inc(consts_ready, 1)
            dve.wait_ge(exps_ready, 2)
            dve.wait_ge(feats_out, 2 + NB)
            f3 = obuf[:].rearrange("p (b x d) -> p b x d", b=NB, d=DH)
            v3 = v18.rearrange("p t h k -> p (t h) k")
            with dve.Fori(0, NB // 2) as b2:
                for i in range(2):
                    b = b2 * 2 + i
                    kb = Count(b2 * (2 * K_BLOCK) + (i * K_BLOCK + k.n))
                    dve.wait_ge(cast_done, b2 * 12 + (i * 6 + 6))
                    for half, e in enumerate((e1, e2)):
                        eb = e.rearrange("p (b t) h -> p b (t h)", b=NB)[:, b, :].unsqueeze(2)
                        lo = half * VC
                        dve.tensor_tensor(v3[:, :, lo:lo + DH], f3[:, b, :, :],
                                          eb.to_broadcast([P, BT * H, DH]), ALU.mult
                                          ).then_inc(dve_step, kb.up())
                        last = dve.tensor_scalar(v3[:, :, lo + DH:lo + VC], eb, 1.0, None, ALU.mult)
                        if half == 0:
                            last.then_inc(dve_step, kb.up())
                    last.then_inc(rest_ready, 1)
                    for s in range(SPLIT - 1):
                        dve.wait_ge(dve_step, kb.now())
                        dve.wait_ge(rest_ready, b2 * 6 + (i * 3 + s + 1))
                        dve.wait_ge(cast_done, b2 * 12 + (i * 6 + s * 2 + 8))
                        for g in range(NG):
                            hs = slice(g * GH, (g + 1) * GH)
                            part = wst[i][:, g, :, AVP:].rearrange("p t (h w) -> p t h w", h=GH)[
                                :, :, :, s * 2 * VC:(s + 1) * 2 * VC]
                            rest = dve.tensor_tensor(v18[:, :, hs, :], v18[:, :, hs, :], part, ALU.subtract)
                            if g == 0:
                                rest.then_inc(dve_step, kb.up())
                        rest.then_inc(rest_ready, 1)
                    assert kb.n == K_BLOCK, kb.n
            k.n += NB * K_BLOCK
            for i in range(2):
                dve.wait_ge(w_stored[i], 16 + 8 * NB)
            k0 = k.n

            def post(it):
                kp = Count(it * K_POST + k0)
                dve.wait_ge(z_ready, it + 2)
                masked_sums = z0[:, :, 0:2 * GH * VC].rearrange("p m (h k) -> p m h k", h=GH)
                all_sums = z0[:, :, 2 * GH * VC:3 * GH * VC].rearrange("p m (h k) -> p m h k", h=GH)
                dve.tensor_copy(t1[:], all_sums).then_inc(dve_step, kp.up())
                dve.tensor_scalar(rdeg[:, it, :], z0[:, :, 3 * GH * VC], 1.0, None, ALU.add
                                  ).then_inc(dve_step, kp.up())
                dve.wait_ge(dve_step, kp.now())
                dve.tensor_tensor(t1[:], t1[:], masked_sums[:, :, :, VC:2 * VC], ALU.subtract
                                  ).then_inc(dve_step, kp.up())
                dve.wait_ge(dve_step, kp.now())
                dve.wait_ge(bn_ready, 1)
                dve.tensor_tensor(t1[:], t1[:], bn[:, it, :, :].unsqueeze(3).to_broadcast([P, CT, GH, VC]),
                                  ALU.mult).then_inc(dve_step, kp.up())
                dve.wait_ge(dve_step, kp.now())
                dve.tensor_tensor(t1[:], t1[:], masked_sums[:, :, :, 0:VC], ALU.add).then_inc(z_used, 1)
                dve.wait_ge(z_used, it + 2)
                dve.reciprocal(rden[:], t1[:, :, :, DH]).then_inc(dve_step, kp.up())
                dve.wait_ge(dve_step, kp.now())
                dve.tensor_tensor(o_it[:, it, :, :].rearrange("p m (h d) -> p m h d", h=GH),
                                  t1[:, :, :, 0:DH], rden[:].unsqueeze(3).to_broadcast([P, CT, GH, DH]),
                                  ALU.mult).then_inc(dve_step, kp.up())
                assert kp.n == K_POST, kp.n

            def attention_step(it, behind):
                dve.wait_ge(cmp_v, it * V_CMP + 1)
                dve.tensor_scalar(thr[:], nthr[:, it % 2, :, :], 1.0, None, ALU.mult).then_inc(thr_ready, 1)
                dve.wait_ge(thr_ready, it + 1)
                made_v, made_s = [0], [0]
                for jt in range(T + 1):
                    if jt < T:
                        dve.wait_ge(tiles_done, it * T + (CREDIT + jt + 1 - RING))
                        for h in dve_heads(jt):
                            if jt == 0:
                                dve.wait_ge(s_loaded[h], it * 16 + 16)
                            dve.tensor_scalar(masks[:, jt % RING, h, :, :].rearrange("p f k -> p (f k)"),
                                              srow[:, h, :], thr[:, jt, h:h + 1], ONE8, ALU.is_gt, ALU.mult
                                              ).then_inc(cmp_v, 1)
                        made_v.append(made_v[-1] + len(dve_heads(jt)))
                        made_s.append(made_s[-1] + GH - len(dve_heads(jt)))
                    if jt > 0:
                        j = jt - 1
                        b, t = j // BT, j % BT
                        if t == 0:
                            dve.wait_ge(a_loaded[b], chunk_of(it) * 16 + 16)
                        dve.wait_ge(cmp_v, it * V_CMP + (1 + made_v[jt]))
                        dve.wait_ge(cmp_s, it * S_CMP + (1 + made_s[jt]))
                        m = masks16[:, j % RING, :, :, :]
                        dve.tensor_tensor(m, m, a16[:, b, :, t, :].unsqueeze(1).to_broadcast(
                            [P, GH, 2, HALF // 2]), ALU.bitwise_and).then_inc(masked, 1)
                    if behind and jt == 8:
                        post(it - 1)
                dve.wait_ge(tiles_done, it * T + (CREDIT + T))
                dve.wait_ge(z_ready, it + 1)
                for bank in (0, 2, 4):
                    rows = AVC if bank % 3 == 2 else P
                    dve.tensor_copy(drained[0:rows, bank, :], ps[0:rows, bank, :]).then_inc(drained_v, 1)

            attention_step(0, False)
            with dve.Fori(1, IT) as it:
                attention_step(it, True)
            post(IT - 1)
            k = Count(k0 + IT * K_POST)
            dve.wait_ge(dve_step, k.now())
            dve.reciprocal(rdeg[:], rdeg[:]).then_inc(dve_step, k.up())
            dve.tensor_copy(ident[:], identf[:]).then_inc(consts_ready, 1)
            dve.tensor_scalar(rx[:], rx[:], 1.0 / VS, None, ALU.mult).then_inc(consts_ready, 1)
            dve.tensor_scalar(wa[:], wa[:], 1.0 / VS, None, ALU.mult).then_inc(consts_ready, 1)
            dve.tensor_scalar(wb[:], wb[:], 1.0 / VS, None, ALU.mult).then_inc(consts_ready, 1)
            dve.tensor_scalar(sel2[:], sel2[:], 1.0 / VS, None, ALU.mult).then_inc(consts_ready, 1)
            for i in range(2):
                dve.tensor_tensor(gb[:, i, 0:2 * D], gb[:, i, 0:2 * D], gb2[:, i, :], ALU.add
                                  ).then_inc(consts_ready, 1)
            dve.wait_ge(x_in, 16)
            dve.wait_ge(dve_step, k.now())
            dve.wait_ge(cmp_s, IT * S_CMP + 1)

            def per_row(a):
                return a.unsqueeze(2).to_broadcast([P, HT, D])

            def norm(kk):
                mean, var, seed, half, y = (st[:, i, :] for i in range(5))
                dve.wait_ge(dve_step, kk.now())
                dve.tensor_reduce(mean, u[:], AX.X, ALU.add).then_inc(dve_step, kk.up())
                dve.wait_ge(dve_step, kk.now())
                dve.tensor_scalar(mean, mean, 1.0 / D, None, ALU.mult).then_inc(dve_step, kk.up())
                dve.wait_ge(dve_step, kk.now())
                dve.tensor_tensor(u[:], u[:], per_row(mean), ALU.subtract).then_inc(dve_step, kk.up())
                dve.wait_ge(dve_step, kk.now())
                dve.tensor_tensor(q[:], u[:], u[:], ALU.mult).then_inc(dve_step, kk.up())
                dve.wait_ge(dve_step, kk.now())
                dve.tensor_reduce(var, q[:], AX.X, ALU.add).then_inc(dve_step, kk.up())
                dve.wait_ge(dve_step, kk.now())
                dve.tensor_scalar(var, var, 1.0 / D, EPS, ALU.mult, ALU.add).then_inc(dve_step, kk.up())
                dve.wait_ge(dve_step, kk.now())
                dve.tensor_scalar(seed.bitcast(I32), var.bitcast(I32), 1, None, ALU.logical_shift_right
                                  ).then_inc(dve_step, kk.up())
                dve.tensor_scalar(half, var, -0.5, None, ALU.mult).then_inc(dve_step, kk.up())
                dve.wait_ge(dve_step, kk.now())
                dve.tensor_scalar(y.bitcast(I32), seed.bitcast(I32), -1.0, float(0x5f3759df),
                                  ALU.mult, ALU.add).then_inc(dve_step, kk.up())
                for _ in range(3):
                    dve.wait_ge(dve_step, kk.now())
                    dve.tensor_tensor(seed, y, y, ALU.mult).then_inc(dve_step, kk.up())
                    dve.wait_ge(dve_step, kk.now())
                    dve.tensor_tensor(seed, seed, half, ALU.mult).then_inc(dve_step, kk.up())
                    dve.wait_ge(dve_step, kk.now())
                    dve.scalar_tensor_tensor(out=y, in0=seed, scalar=1.5, in1=y, op0=ALU.add, op1=ALU.mult
                                             ).then_inc(dve_step, kk.up())
                dve.wait_ge(dve_step, kk.now())
                dve.tensor_tensor(u[:], u[:], per_row(y), ALU.mult).then_inc(dve_step, kk.up())
                dve.wait_ge(dve_step, kk.now())

            def split(kk, src, dst, hf, keep):
                high, low = dst[:, hf, :, 0:D], dst[:, hf, :, D:2 * D]
                dve.tensor_scalar(keep[:, hf, :, :], src, 1.0, None, ALU.mult).then_inc(dve_step, kk.up())
                dve.tensor_scalar(high, src, VS, None, ALU.mult).then_inc(dve_step, kk.up())
                dve.tensor_scalar(q[:], src, VS, None, ALU.mult).then_inc(dve_step, kk.up())
                dve.wait_ge(dve_step, kk.now())
                dve.tensor_tensor(low, q[:], high, ALU.subtract).then_inc(v_ready, 1)

            k0 = k.n + k.base
            with dve.Fori(0, NC) as c:
                for f in range(2):
                    hf = c * 2 + f
                    kk = Count(c * (2 * K_FIRST) + (f * K_FIRST + k0))
                    if f == 1:
                        dve.wait_ge(v_ready, hf)
                    for g in range(NG):
                        dve.tensor_tensor(u[:, :, g * 32:(g + 1) * 32],
                                          o_it[:, c * 2 + g, f * HT:(f + 1) * HT, :],
                                          b0[:, g * 32:(g + 1) * 32].unsqueeze(1).to_broadcast([P, HT, 32]),
                                          ALU.add).then_inc(dve_step, kk.up())
                    dve.wait_ge(dve_step, kk.now())
                    dve.tensor_scalar(u[:], u[:], 0.0, None, ALU.max).then_inc(dve_step, kk.up())
                    dve.wait_ge(dve_step, kk.now())
                    dve.tensor_tensor(u[:], u[:], x_hf[:, hf, :, :], ALU.add).then_inc(dve_step, kk.up())
                    norm(kk)
                    split(kk, u[:], vals[0], hf, x_hf)
                    assert kk.n == K_FIRST, kk.n
            k0 += NH * K_FIRST

            def epilogue(p, c, f, k0):
                hf = c * 2 + f
                n = c * 2 + ((p - 1) * NH + f)
                kk = Count(c * (2 * K_PASS[p]) + (f * K_PASS[p] + k0))
                z = zz[f]
                if p < 4:
                    dve.wait_ge(v_ready, n + NH)
                else:
                    dve.wait_ge(row_out, c * 2 + (f + 1))
                dve.wait_ge(zz_ready, n + 1)
                if p == 1:
                    dot = st[:, 5, :]
                    dve.tensor_tensor(q[:], z[:, :, 0:D], x_hf[:, hf, :, :], ALU.mult).then_inc(zz_used, 1)
                    dve.wait_ge(zz_used, n + 2)
                    dve.tensor_reduce(dot, q[:], AX.X, ALU.add).then_inc(dve_step, kk.up())
                    dve.tensor_scalar(u[:], x_hf[:, hf, :, :], -0.1, None, ALU.mult).then_inc(dve_step, kk.up())
                    dve.wait_ge(dve_step, kk.now())
                    dve.tensor_scalar(dot, dot, -0.01, 1.0, ALU.mult, ALU.add).then_inc(dve_step, kk.up())
                    dve.wait_ge(dve_step, kk.now())
                    dve.tensor_tensor(u[:], u[:], per_row(dot), ALU.add).then_inc(dve_step, kk.up())
                    dve.wait_ge(dve_step, kk.now())
                    dve.tensor_tensor(u[:], u[:], x_hf[:, hf, :, :], ALU.add).then_inc(dve_step, kk.up())
                    norm(kk)
                    split(kk, u[:], vals[1], hf, x_hf)
                elif p < 4:
                    xin = x_hf if p == 2 else h_hf
                    dve.tensor_tensor(gates, z, gb[:, p - 2, :].unsqueeze(1).to_broadcast([P, HT, GATES]),
                                      ALU.add).then_inc(zz_used, 1)
                    dve.wait_ge(gates_out, n - (NH - 1))
                    dve.tensor_tensor(nn[:], gates[:, :, 0:D], gates[:, :, 2 * D:3 * D], ALU.mult
                                      ).then_inc(dve_step, kk.up())
                    dve.wait_ge(dve_step, kk.now())
                    dve.tensor_tensor(nn[:], nn[:], gates[:, :, 3 * D:4 * D], ALU.add).then_inc(cand_in, 1)
                    dve.wait_ge(cand_out, n - (NH - 1))
                    dve.tensor_tensor(hh[:], xin[:, hf, :, :], nn[:], ALU.subtract).then_inc(dve_step, kk.up())
                    dve.wait_ge(dve_step, kk.now())
                    dve.tensor_tensor(hh[:], hh[:], gates[:, :, D:2 * D], ALU.mult).then_inc(dve_step, kk.up())
                    dve.wait_ge(dve_step, kk.now())
                    dve.tensor_tensor(hh[:], hh[:], nn[:], ALU.add).then_inc(dve_step, kk.up())
                    dve.wait_ge(dve_step, kk.now())
                    dve.tensor_scalar(hh[:], hh[:], 0.0, None, ALU.max).then_inc(dve_step, kk.up())
                    dve.wait_ge(dve_step, kk.now())
                    if p == 2:
                        split(kk, hh[:], vals[0], hf, h_hf)
                    else:
                        dve.tensor_tensor(u[:], hh[:], x_hf[:, hf, :, :], ALU.add).then_inc(dve_step, kk.up())
                        norm(kk)
                        split(kk, u[:], vals[1], hf, x_hf)
                else:
                    own = rdeg[:, c * 2, f * HT:(f + 1) * HT]
                    dve.tensor_tensor(u[:], z[:, :, D:2 * D], per_row(own), ALU.mult).then_inc(dve_step, kk.up())
                    dve.wait_ge(dve_step, kk.now())
                    dve.tensor_tensor(u[:], u[:], z[:, :, 0:D], ALU.add).then_inc(zz_used, 1)
                    dve.wait_ge(zz_used, n + 2)
                    dve.tensor_tensor(u[:], u[:], x_hf[:, hf, :, :], ALU.add).then_inc(dve_step, kk.up())
                    norm(kk)
                    dve.tensor_scalar(h_hf[:, hf, :, :], u[:], 1.0, None, ALU.mult).then_inc(row_out, 1)
                assert kk.n == K_PASS[p], (p, kk.n)

            for p in range(1, 5):
                with dve.Fori(0, NC) as c:
                    for f in range(2):
                        epilogue(p, c, f, k0)
                k0 += NH * K_PASS[p]


_F32_INPUTS = ("adj", "xT", "xN", "W0", "attS", "attN", "bias0", "W1T", "wihT", "whhT", "bih", "bhh", "W3T",
               "consts")


def kernel(**inputs):
    import numpy as np
    import concourse.bacc as bacc
    from concourse.bass_utils import run_bass_kernel_spmd

    a = {k: np.asarray(v) for k, v in inputs.items()}

    add_pairs = np.zeros((P, 4 * VC), np.float32)
    for h in range(2):
        for s in range(SPLIT):
            for c in range(2 * VC):
                add_pairs[h * HW + s * 2 * VC + c, h * 2 * VC + c] = 1
    add_all = np.zeros((P, GH * VC + 1), np.float32)
    for s in range(SPLIT):
        for c in range(GH * VC):
            add_all[s * GH * VC + c, c] = 1
    add_all[AVC - 1, GH * VC] = 1
    eye = np.eye(P, dtype=np.float32)
    add_two = np.concatenate([eye[:D, :D], eye[:D, :D]])

    x, adj = a["x"], a["adj"]
    arrays = {
        "adj": np.ascontiguousarray(
            adj.reshape(NC, 2, HALF, NB, BT, P).transpose(0, 3, 5, 1, 4, 2)).reshape(NC, NB, P, -1),
        "xT": np.ascontiguousarray(x.T),
        "xN": np.ascontiguousarray(x.reshape(T, P, D).transpose(1, 0, 2)).reshape(P, T * D),
        "W0": a["L0_gnn_W"],
        "attS": a["L0_gnn_att_self"].reshape(D),
        "attN": a["L0_gnn_att_neigh"].reshape(D),
        "bias0": a["L0_gnn_bias"].reshape(D),
        "W1T": np.stack([a["L2_gnn_W1"].T, a["L2_gnn_W2"].T]),
        "wihT": np.stack([a["L2_gnn_wih1"].T, a["L2_gnn_wih2"].T]),
        "whhT": np.stack([a["L2_gnn_whh1"].T, a["L2_gnn_whh2"].T]),
        "bih": np.stack([a["L2_gnn_bih1"], a["L2_gnn_bih2"]]),
        "bhh": np.stack([a["L2_gnn_bhh1"], a["L2_gnn_bhh2"]]),
        "W3T": np.ascontiguousarray(a["L3_gnn_W"].T),
        "consts": np.concatenate([eye, add_pairs, add_all, add_two], axis=1),
    }
    nc = bacc.Bacc("TRN2", target_bir_lowering=False, num_devices=1)
    sent = {f"in_{k}": np.ascontiguousarray(arrays[k]) for k in _F32_INPUTS}
    aps = [nc.dram_tensor(k, v.shape, F32, kind="ExternalInput").ap() for k, v in sent.items()]
    out = nc.dram_tensor("out", (P, NH, HT * D), F32, kind="ExternalOutput").ap()
    build(nc, *aps, out)
    r = run_bass_kernel_spmd(nc, [sent], core_ids=[0])
    return np.ascontiguousarray(
        r.results[0]["out"].reshape(P, T, D).transpose(1, 0, 2)).reshape(N, D)
```

```python
from contextlib import ExitStack

import concourse.bass as bass
from concourse import mybir

F32, BF16, F16 = mybir.dt.float32, mybir.dt.bfloat16, mybir.dt.float16
F8, U8, U16, I32, U32 = (mybir.dt.float8e4, mybir.dt.uint8, mybir.dt.uint16, mybir.dt.int32,
                         mybir.dt.uint32)
ALU = mybir.AluOpType
ACT = mybir.ActivationFunctionType
AX = mybir.AxisListType

P = 128
N, D, H = 8192, 64, 8
DH = D // H
T = N // P
CH, HALF = 1024, 512
NC = N // CH
NH = N // HALF
BT = 8
NB = T // BT
CT = CH // P
HT = HALF // P
NG, GH = 2, 4
IT = NC * NG
VC = DH + 1
SPLIT = 3
EW = 32
HW = 2 * EW
E2_AT = EW
ONES_AT = 2 * EW - 1
WC = GH * HW
RING = 6
WSLOTS = 4
CREDIT = 32
BIG = float(2 ** 40)
ONE8 = 56.0
VS = 4096.0
EPS = 1e-5
QT = T // 4
GATES = 256
BANKS = 6


def dve_heads(jt):
    return [0] if jt % 4 == 3 or jt % 16 == 9 else [0, 1]


def slot_free(jt):
    return CREDIT + (jt - RING if jt >= RING else (T - 1 - jt) // RING * RING + jt - T) + 1


K_BLOCK, K_POST, K_FIRST = 3, 6, 22
K_PASS = {1: 23, 2: 6, 3: 24, 4: 19}
NORM_STEPS = 16


V_CMP = sum(len(dve_heads(j)) for j in range(T))
S_CMP = GH * T - V_CMP


class Count:

    def __init__(self, base):
        self.base, self.n = base, 0

    def up(self):
        self.n += 1
        return 1

    def now(self):
        return self.base + self.n


def build(nc, adj, xT, xN, W0, attS, attN, bias0, W1T, wihT, whhT, bih, bhh, W3T, consts, out):
    with ExitStack() as ctx:
        def sb(name, shape, dt):
            return ctx.enter_context(nc.sbuf_tensor(name, shape, dt))

        def sem(name):
            return ctx.enter_context(nc.semaphore(name))

        adj8 = nc.dram_tensor("adj8", (NH, 4, P, 2, BT * HALF), U8, kind="Internal").ap()
        w_tab = nc.dram_tensor("w_tab", (NG, NB, P, BT * WC), BF16, kind="Internal").ap()
        s_rows = nc.dram_tensor("s_rows", (NC, H, CH), F32, kind="Internal").ap()

        abuf = sb("abuf", [P, NB, 2, BT, HALF], U8)
        a8 = abuf[:].bitcast(F8)
        a16 = abuf[:].bitcast(U16)
        wring = sb("wring", [P, WSLOTS, BT, WC], BF16)
        early = sb("early", [P, GH * CH * 4 + RING * GH * CH], U8)
        masks = early[:, GH * CH * 4:].rearrange("p (s h f k) -> p s h f k", s=RING, h=GH, f=2)
        masks8 = masks.bitcast(F8)
        masks16 = masks.bitcast(U16)
        VB = T * P * 2
        vals0 = sb("vals0", [P, T * P], F16)
        vals = [v.rearrange("p (f m k) -> p f m k", f=NH, m=HT)
                for v in (vals0[:], early[:, 0:VB].bitcast(F16))]
        vals_ch = vals0[:].rearrange("p (c m k) -> p c m k", c=NC, m=CT)
        stage_at = GH * CH * 4
        WST = NG * BT * WC * 2
        wst = [early[:, stage_at + i * WST:stage_at + (i + 1) * WST].bitcast(BF16) for i in range(2)]
        wst_parts = [w.rearrange("p (x e) -> p x e", e=EW) for w in wst]
        gbuf = sb("gbuf", [P, BANKS * HALF * 4], U8)
        drained = gbuf[:].bitcast(F32).rearrange("p (b k) -> p b k", b=BANKS)
        VBLOCK = BT * H * 2 * VC
        v18 = [gbuf[:, i * VBLOCK * 4:(i + 1) * VBLOCK * 4].bitcast(F32) for i in range(2)]
        ybuf = [drained[:, i, :] for i in range(2)]
        xt_sb = drained[:, 2, :]
        gates = gbuf[:, 3 * 2048:5 * 2048].bitcast(F32).rearrange("p (m k) -> p m k", m=HT)
        xbuf = sb("xbuf", [P, T * D], F32)
        x_hf = xbuf[:].rearrange("p (f m d) -> p f m d", f=NH, m=HT)
        x_ch = xbuf[:].rearrange("p (c m d) -> p c m d", c=NC, m=CT)
        s_self = xbuf[:, 0:512].rearrange("p (t h) -> p t h", t=T)
        s_neigh, dd, fac0, fac1 = (xbuf[:, 512 * i:512 * (i + 1)].rearrange("p (g t h) -> p g t h", g=NG, t=T)
                                   for i in range(1, 5))
        obuf = sb("obuf", [P, T * D], F32)
        feats = obuf[:].rearrange("p (b g t c) -> p b g t c", b=NB, g=NG, t=BT)
        h_hf = obuf[:].rearrange("p (f m d) -> p f m d", f=NH, m=HT)
        srow = [a.rearrange("p (h r) -> p h r", h=GH) for a in (early[:, 0:GH * CH * 4].bitcast(F32), obuf[:])]
        o_now = sb("o_now", [P, NG, CT, GH * DH], F32)
        xT_sb = abuf[0:D, NB // 2:, :, :, :].rearrange("p a b c d -> p (a b c d)").bitcast(F32)
        srowT = gbuf[:, 9216:9216 + 2048].bitcast(F32).rearrange("p (q k) -> p q k", q=4)
        bn = sb("bn", [P, IT, CT, GH], F32)
        nthr = sb("nthr", [P, NG, T, GH], F32)
        nbig = sb("nbig", [P, NG, T, GH], F32)
        rdeg = sb("rdeg", [P, IT, CT], F32)
        t1 = sb("t1", [P, CT, GH, VC], F32)
        rden = sb("rden", [P, CT, GH], F32)
        u_ch = sb("u", [P, CT, D], F32)
        q_ch = sb("q", [P, CT, D], F32)
        st_ch = sb("st", [P, 6, CT], F32)
        u, q, st = u_ch[:, 0:HT, :], q_ch[:, 0:HT, :], st_ch[:, :, 0:HT]
        nn = sb("nn", [P, HT, D], F32)
        hh = sb("hh", [P, HT, D], F32)
        wcat = sb("wcat", [D, 16 + D], F32)
        att, wtmp = nn[0:D, 0:2, :], hh[0:D, 0:2, :]
        b0 = sb("b0", [P, D], F32)
        selP = sb("selP", [P, 2 * 2 * VC], F32)
        selA = sb("selA", [P, GH * VC + 1], F32)
        sel2 = sb("sel2", [P, D], F32)
        identf = sb("identf", [P, P], F32)
        ident = sb("ident", [P, P], F16)
        nmax = sb("nmax", [P, H], F32)
        nall = sb("nall", [P, H], F32)
        w1t = sb("w1t", [D, 2, 2, D], F32)
        wih = sb("wih", [D, 2, 3 * D], F32)
        rx = sb("rx", [P, 2, 3 * D], F32)
        ry = sb("ry", [P, 2, 3 * D], F32)
        gb = sb("gb", [P, 2, GATES], F32)
        gb2 = sb("gb2", [P, 2, 2 * D], F32)
        wa = sb("wa", [P, D], F32)
        wb = sb("wb", [P, D], F32)

        ps = ctx.enter_context(nc.psum_tensor("ps", [P, 8, HALF], F32))
        first = [ps[:, 2 * i:2 * i + 2, :].rearrange("p b (t k) -> p (b t) k", k=P) for i in range(4)]
        z0 = ps[:, 6:8, :].rearrange("p b (m k) -> p (b m) k", m=4)
        zz = [ps[:, 4 + 2 * i:6 + 2 * i, :].rearrange("p b (m k) -> p (b m) k", m=2) for i in range(2)]

        params = sem("params")
        w0_in = sem("w0_in")
        xT_in = [sem(f"xT_in{i}") for i in range(4)]
        x_in = sem("x_in")
        watt_ready = sem("watt_ready")
        first_ready = sem("first_ready")
        first_v = sem("first_v")
        first_s = sem("first_s")
        turned = sem("turned")
        turned_out = sem("turned_out")
        rows_stored = sem("rows_stored")
        nmax_ready = sem("nmax_ready")
        nall_ready = sem("nall_ready")
        dd_ready = sem("dd_ready")
        exps_ready = sem("exps_ready")
        relu_ready = sem("relu_ready")
        bn_ready = sem("bn_ready")
        zeroed = sem("zeroed")
        cast_done = sem("cast_done")
        rest_ready = sem("rest_ready")
        w_stored = [sem(f"w_stored{i}") for i in range(2)]
        dve_step = sem("dve_step")
        a_loaded = [sem(f"a_loaded{b}") for b in range(NB)]
        a_stored = [sem(f"a_stored{b}") for b in range(NB)]
        w_loaded = [sem(f"w_loaded{k}") for k in range(WSLOTS)]
        s_loaded = [sem(f"s_loaded{g}") for g in range(NG)]
        cmp_v = sem("cmp_v")
        cmp_s = sem("cmp_s")
        masked = sem("masked")
        tiles_done = sem("tiles_done")
        drained_v = sem("drained_v")
        drained_s = sem("drained_s")
        z_ready = sem("z_ready")
        z_used = sem("z_used")
        gate = sem("gate")
        ry_ready = sem("ry_ready")
        consts_ready = sem("consts_ready")
        v_ready = sem("v_ready")
        q_loaded = [sem(f"q_loaded{k}") for k in range(8)]
        q_done = sem("q_done")
        y_out = sem("y_out")
        xt_ready = sem("xt_ready")
        xt_out = sem("xt_out")
        xz_done = sem("xz_done")
        zz_ready = sem("zz_ready")
        zz_used = sem("zz_used")
        gates_out = sem("gates_out")
        cand_in = sem("cand_in")
        cand_out = sem("cand_out")
        row_out = sem("row_out")
        stored = sem("stored")

        block = ctx.enter_context(nc.Block())

        def lead(eng):
            eng.sem_inc(gate, 1)

        n_small = 5 + 2 * (1 + 6 + 4) + 4

        @block.sync
        def _(sp):
            def small(dst, src):
                sp.dma_start(dst, src).then_inc(params, 16)

            sp.dma_start(wcat[:, 16:], W0).then_inc(w0_in, 16)
            sp.dma_start(att[:, 0, :], attS.partition_broadcast(D)).then_inc(w0_in, 16)
            sp.dma_start(att[:, 1, :], attN.partition_broadcast(D)).then_inc(w0_in, 16)
            for i in range(4):
                cols = slice(i * (N // 4), (i + 1) * (N // 4))
                sp.dma_start(xT_sb[:, cols], xT[:, cols]).then_inc(xT_in[i], 16)
            small(b0[:], bias0.partition_broadcast(P))
            small(identf[:], consts[:, 0:P])
            small(selP[:], consts[:, P:P + 36])
            small(selA[:], consts[:, P + 36:P + 73])
            small(sel2[:], consts[:, P + 73:P + 73 + D])
            for k in range(2):
                small(wih[:, k, :], wihT[k])
                for r in range(2):
                    small(w1t[:, k, r, :], W1T[k])
                    small(rx[r * D:(r + 1) * D, k, D:3 * D], whhT[k][:, 0:2 * D])
                    small(rx[r * D:(r + 1) * D, k, 0:D], whhT[k][:, 2 * D:3 * D])
                small(gb[:, k, D:3 * D], bih[k, 0:2 * D].partition_broadcast(P))
                small(gb2[:, k, :], bhh[k, 0:2 * D].partition_broadcast(P))
                small(gb[:, k, 0:D], bhh[k, 2 * D:3 * D].partition_broadcast(P))
                small(gb[:, k, 3 * D:4 * D], bih[k, 2 * D:3 * D].partition_broadcast(P))
            for r in range(2):
                small(wa[r * D:(r + 1) * D, :], W3T[0:D, :])
                small(wb[r * D:(r + 1) * D, :], W3T[D:2 * D, :])
            for k in range(4):
                sp.wait_ge(turned_out, k + 1)
                lead(sp)
                for c in range(2):
                    sp.dma_start(s_rows[2 * k + c].rearrange("h (m p) -> m h p", p=P),
                                 srowT[c * D:(c + 1) * D, k, :]).then_inc(rows_stored, 16)
            with sp.Fori(0, NB // 2) as k:
                for i in range(2):
                    sp.wait_ge(cast_done, k * 6 + (11 + i))
                    lead(sp)
                    sp.dma_start(w_tab[:, k * 2 + i, :, :].rearrange("g p w -> p g w"),
                                 wst[i].rearrange("p (g w) -> p g w", g=NG)).then_inc(w_stored[i], 16)
            sp.wait_ge(rows_stored, 16 * 8)
            for i in range(2):
                sp.wait_ge(w_stored[i], 16 + 8 * NB)
            with sp.Fori(0, NC) as c:
                for g in range(NG):
                    for b in range(NB):
                        sp.wait_ge(tiles_done,
                                   c * (NG * T) + (g * T + CREDIT + (b - WSLOTS + 1) * BT))
                        lead(sp)
                        sp.dma_start(wring[:, b % WSLOTS, :, :].rearrange("p t w -> p (t w)"),
                                     w_tab[g, b, :, :]).then_inc(w_loaded[b % WSLOTS], 16)
                        if b == 0:
                            sp.dma_start(srow[g], s_rows[c, g * GH:(g + 1) * GH, :].partition_broadcast(P)
                                         ).then_inc(s_loaded[g], 16)
                        if g == 0:
                            sp.wait_ge(a_loaded[b], c * 16 + 16)
                            lead(sp)
                            sp.dma_start(
                                adj8[bass.ds(c * 2, 2), b // 2, :, b % 2, :].rearrange("f p k -> p f k"),
                                abuf[:, b, :, :, :].rearrange("p f t k -> p f (t k)")
                            ).then_inc(a_stored[b], 16)

            def load_adj8(c, slot):
                sp.dma_start(abuf[:, slot, :, :, :].rearrange("p f t k -> p (f t k)"),
                             adj8[c * 2 + slot // 4, slot % 4, :, :, :].rearrange("p b k -> p (b k)")
                             ).then_inc(q_loaded[slot], 16)

            for b in range(NB):
                sp.wait_ge(a_stored[b], 16 * NC)
            for slot in range(8):
                sp.wait_ge(tiles_done, CREDIT + (IT - 1) * T + (slot + 1) * BT)
                load_adj8(0, slot)
            for p in range(4):
                with sp.Fori(1 if p == 0 else 0, NC) as c:
                    for slot in range(8):
                        sp.wait_ge(q_done, c * 8 + (p * 64 + slot + 1))
                        lead(sp)
                        load_adj8(c, slot)
            with sp.Fori(0, NH) as n:
                sp.wait_ge(row_out, n + 2)
                lead(sp)
                sp.dma_start(out[:, n, :], h_hf[:, n, :, :].rearrange("p m d -> p (m d)")
                             ).then_inc(stored, 16)
            sp.wait_ge(stored, 16 * NH)

        @block.gpsimd
        def _(pool):
            def load_adj(c, b):
                pool.dma_start(a8[:, b, :, :, :].rearrange("p f t k -> p (f t k)"),
                               adj[c, b, :, :]).then_inc(a_loaded[b], 16)

            for i in range(2):
                pool.memset(wst[i].bitcast(U32), 0).then_inc(zeroed, 1)
            pool.wait_ge(zeroed, 2)
            for i in range(2):
                pool.memset(wst[i].rearrange("p (x w) -> p x w", w=2 * HW)[:, :, ONES_AT:ONES_AT + 1], 1.0
                            ).then_inc(zeroed, 1)
            for i in range(4):
                pool.wait_ge(xT_in[i], 16)
            for b in range(NB // 2):
                load_adj(0, b)
            pool.wait_ge(nmax_ready, 1)
            pool.partition_all_reduce(nall[:], nmax[:], P, bass.bass_isa.ReduceOp.max).then_inc(nall_ready, 1)
            pool.wait_ge(first_ready, NB)
            for b in range(NB // 2, NB):
                load_adj(0, b)
            pool.wait_ge(rest_ready, 3 * NB)
            pool.dma_start(xbuf[:], xN).then_inc(x_in, 16)
            for c in range(1, NC):
                for b in range(NB):
                    pool.wait_ge(tiles_done, CREDIT + (2 * c - 1) * T + (b + 1) * BT)
                    pool.wait_ge(a_stored[b], 16 * c)
                    load_adj(c, b)

        @block.tensor
        def _(pe):
            pe.sem_inc(tiles_done, CREDIT)
            pe.sem_inc(z_ready, 1)
            pe.sem_inc(q_done, 8)
            pe.wait_ge(w0_in, 48)
            pe.wait_ge(watt_ready, 2)
            for k in range(NB):
                if k % 2 == 0:
                    pe.wait_ge(xT_in[k // 2], 16)
                if k >= 4:
                    pe.wait_ge((first_s, first_v)[k % 2], 3 * ((k - 4) // 2 + 1))
                for m in range(8):
                    mm = pe.matmul(first[k % 4][:, m, 0:16 + D],
                                   xT_sb[:, (k * 8 + m) * P:(k * 8 + m + 1) * P], wcat[:],
                                   start=True, stop=True)
                mm.then_inc(first_ready, 1)
            pe.wait_ge(first_s, 3 * NB // 2)
            pe.wait_ge(first_v, 3 * NB // 2)
            pe.wait_ge(params, 16 * n_small)
            for k in range(4):
                pe.matmul(ps[:, 2 + k, 0:P], xbuf[:, k * P:(k + 1) * P], identf[:],
                          start=True, stop=True).then_inc(turned, 1)
            for k in range(2):
                mm = pe.matmul(ps[:, 0, k * 192:(k + 1) * 192], w1t[:, k, :, :].rearrange("p r d -> p (r d)"),
                               wih[:, k, :], start=True, stop=True)
            mm.then_inc(ry_ready, 1)
            pe.wait_ge(turned_out, 4)
            pe.wait_ge(consts_ready, 1)

            def tile_sums(it, b, t):
                jt = b * BT + t
                ws = wring[:, b % WSLOTS, t, :]
                if t == 0:
                    pe.wait_ge(w_loaded[b % WSLOTS], it * 32 + (16 * (b // WSLOTS) + 16))
                    lead(pe)
                pe.wait_ge(masked, it * T + (jt + 1))
                lead(pe)
                for f in range(2):
                    for h in range(GH):
                        r = (h % 2) * HW
                        pe.matmul(ps[r:r + HW, f * 3 + h // 2, :], ws[:, h * HW:(h + 1) * HW],
                                  masks8[:, jt % RING, h, f, :], start=(jt == 0), stop=(jt == T - 1),
                                  skip_group_check=True)
                    for pair in range(2):
                        r, at = pair * HW, pair * 2 * HW + E2_AT
                        mm = pe.matmul(ps[r:r + HW, f * 3 + 2, :], ws[:, at:at + HW], a8[:, b, f, t, :],
                                       start=(jt == 0), stop=(jt == T - 1), skip_group_check=True)
                mm.then_inc(tiles_done, 1)

            def gather(it):
                pe.wait_ge(drained_v, it * 3 + 6)
                pe.wait_ge(drained_s, it * 3 + 6)
                pe.wait_ge(z_used, it + 1)
                lead(pe)
                for f in range(2):
                    for m in range(HT):
                        for k in range(3):
                            w = GH * VC + 1 if k == 2 else 4 * VC
                            mm = pe.matmul(z0[:, f * HT + m, k * 36:k * 36 + w],
                                           drained[:, f * 3 + k, m * P:(m + 1) * P],
                                           (selA if k == 2 else selP)[:], start=True, stop=True)
                mm.then_inc(z_ready, 1)

            def attention_step(it, behind):
                pe.wait_ge(drained_v, it * 3 + 3)
                pe.wait_ge(drained_s, it * 3 + 3)
                lead(pe)
                for b in range(NB):
                    for t in range(BT):
                        tile_sums(it, b, t)
                        if behind and b == 0 and t == 3:
                            gather(it - 1)

            attention_step(0, False)
            with pe.Fori(1, IT) as it:
                attention_step(it, True)
            gather(IT - 1)
            pe.wait_ge(consts_ready, 8)

            def x_part(p, n, f):
                pe.wait_ge(xt_out, n - (NH - 1))
                pe.wait_ge(zz_used, n)
                lead(pe)
                w, cols = (rx[:, p - 2, :], 3 * D) if p < 4 else (wa[:], D)
                for m in range(HT):
                    mm = pe.matmul(zz[f][:, m, 0:cols], xt_sb[:, m * P:(m + 1) * P], w,
                                   start=(m % 2 == 0), stop=True, skip_group_check=True)
                mm.then_inc(xz_done, 1)

            def y_part(p, n, f, first=False):
                pe.wait_ge(y_out, n + 1)
                if p == 1 and f == 1 and first:
                    pe.wait_ge(z_used, IT + 1)
                if p == 1 and not first:
                    pe.wait_ge(zz_used, n)
                lead(pe)
                for m in range(HT):
                    lhs = ybuf[f][:, m * P:(m + 1) * P]
                    if p == 1:
                        mm = pe.matmul(zz[f][:, m, 0:D], lhs, sel2[:], start=(m % 2 == 0), stop=True,
                                       skip_group_check=True)
                    elif p == 4:
                        mm = pe.matmul(zz[f][:, m, D:2 * D], lhs, wb[:], start=False, stop=True,
                                       skip_group_check=True)
                    else:
                        mm = pe.matmul(zz[f][:, m, D:4 * D], lhs, ry[:, p - 2, :], start=False, stop=True,
                                       skip_group_check=True)
                mm.then_inc(zz_ready, 1)

            def pass_half(p, c, f, behind):
                base = (p - 1) * NH
                n = c * 2 + (base + f)
                first = isinstance(c, int)
                v = vals[(p - 1) % 2]
                if not (first and n < 2):
                    pe.wait_ge(y_out, n - 1)
                    lead(pe)
                for jt in range(T):
                    slot = f * 4 + jt // QT
                    if jt % QT == 0:
                        pe.wait_ge(q_loaded[slot], c * 16 + ((p - 1) * NC * 16 + 16))
                        lead(pe)
                    if first and p == 1 and jt % CT == 0:
                        pe.wait_ge(v_ready, jt // CT + 1)
                    if first and p > 1 and jt % HT == 0:
                        pe.wait_ge(v_ready, NC + base - NH + jt // HT + 1)
                    mm = pe.matmul(ps[:, f, :], v[:, jt // HT, jt % HT, :],
                                   a8[:, slot, (jt % QT) // BT, jt % BT, :],
                                   start=(jt == 0), stop=(jt == T - 1))
                    if jt % QT == QT - 1:
                        mm.then_inc(q_done, 1)
                    if p > 1 and jt == 8:
                        if not (first and n == NH):
                            pe.wait_ge(xt_out, n - NH)
                            lead(pe)
                        for m in range(HT):
                            mm = pe.matmul(ps[:, 2, m * P:(m + 1) * P], v[:, c * 2 + f, m, :], ident[:],
                                           start=True, stop=True)
                        mm.then_inc(xt_ready, 1)
                    if behind and jt == 20:
                        y_part(p, n - 1, 1 - f, first and n == 1)
                    if p > 1 and jt == 56:
                        x_part(p, n, f)

            for p in range(1, 5):
                pass_half(p, 0, 0, False)
                pass_half(p, 0, 1, True)
                with pe.Fori(1, NC) as c:
                    pass_half(p, c, 0, True)
                    pass_half(p, c, 1, True)
                y_part(p, p * NH - 1, 1)

        @block.scalar
        def _(act):
            act.sem_inc(drained_s, 3)
            act.sem_inc(cmp_s, 1)
            for i in range(2):
                act.sem_inc(w_stored[i], 16)
            act.sem_inc(cast_done, 6)
            for k in range(0, NB, 2):
                act.wait_ge(first_ready, k + 1)
                got = first[k % 4]
                act.copy(feats[:, k, :, :, :], got[:, :, 16:16 + D].rearrange("p t (g c) -> p g t c", g=NG)
                         ).then_inc(first_s, 1)
                act.copy(s_self[:, k * 8:(k + 1) * 8, :], got[:, :, 0:H]).then_inc(first_s, 1)
                act.copy(s_neigh[:, :, k * 8:(k + 1) * 8, :],
                         got[:, :, H:2 * H].rearrange("p t (g h) -> p g t h", g=NG)).then_inc(first_s, 1)
            for k in range(4):
                act.wait_ge(turned, k + 1)
                act.copy(srowT[:, k, :], ps[:, 2 + k, 0:P]).then_inc(turned_out, 1)
            act.wait_ge(dd_ready, 1)
            def heads_of(a, odd):
                return a.rearrange("p g t (h two) -> p (g t h) two", two=2)[:, :, odd]

            for odd in range(2):
                act.activation(heads_of((fac0, fac1)[odd], odd), heads_of(dd, odd), ACT.Exp
                               ).then_inc(exps_ready, 1)
                act.activation(heads_of((fac1, fac0)[odd], odd), heads_of(dd, odd), ACT.Exp, scale=0.2
                               ).then_inc(exps_ready, 1)
            act.wait_ge(relu_ready, 1)
            act.activation(bn[:], bn[:], ACT.Exp, scale=-0.8).then_inc(bn_ready, 1)
            act.wait_ge(zeroed, 4)
            with act.Fori(0, NB // 2) as k:
                for s in range(SPLIT):
                    for i in range(2):
                        act.wait_ge(rest_ready, k * 6 + (s * 2 + i + 1))
                        if s == 0:
                            act.wait_ge(w_stored[i], k * 16 + 16)
                        lead(act)
                        act.copy(wst_parts[i][:, :, s * VC:(s + 1) * VC],
                                 v18[i].rearrange("p (x k) -> p x k", k=VC)).then_inc(cast_done, 1)
            for i in range(2):
                act.wait_ge(w_stored[i], 16 + 8 * NB)

            def drain(it):
                act.wait_ge(tiles_done, it * T + (CREDIT + T))
                act.wait_ge(z_ready, it + 1)
                for k in (1, 3, 5):
                    act.copy(drained[:, k, :], ps[:, k, :]).then_inc(drained_s, 1)

            def attention_step(c, g, behind):
                it = c * NG + g
                act.wait_ge(s_loaded[g], c * 16 + 16)
                lead(act)
                for jt in range(T):
                    act.wait_ge(tiles_done, it * T + slot_free(jt))
                    lead(act)
                    for h in range(len(dve_heads(jt)), GH):
                        act.activation(masks8[:, jt % RING, h, :, :].rearrange("p f k -> p (f k)"),
                                       srow[g][:, h, :], ACT.Sigmoid, bias=nbig[:, g, jt, h:h + 1],
                                       scale=BIG, saturate=False).then_inc(cmp_s, 1)
                    if behind and jt == 1:
                        drain(it - 1)

            attention_step(0, 0, False)
            attention_step(0, 1, True)
            with act.Fori(1, NC) as c:
                for g in range(NG):
                    attention_step(c, g, True)
            drain(IT - 1)
            act.wait_ge(z_used, IT + 1)

            def pass_half(p, c, f, first):
                n = c * 2 + ((p - 1) * NH + f)
                if p > 1:
                    act.wait_ge(xt_ready, n - (NH - 1))
                    if not (first and n == NH):
                        act.wait_ge(xz_done, n - NH)
                    act.copy(xt_sb, ps[:, 2, :]).then_inc(xt_out, 1)
                act.wait_ge(q_done, n * 4 + 12)
                if not (first and n < 2):
                    act.wait_ge(zz_ready, n - 1)
                act.copy(ybuf[f], ps[:, f, :]).then_inc(y_out, 1)
                if p in (2, 3):
                    act.wait_ge(zz_used, n + 2)
                    act.activation(gates[:, :, D:3 * D], gates[:, :, D:3 * D], ACT.Sigmoid
                                   ).then_inc(gates_out, 1)
                    act.wait_ge(cand_in, n - (NH - 1))
                    act.activation(nn[:], nn[:], ACT.Tanh).then_inc(cand_out, 1)

            for p in range(1, 5):
                for f in range(2):
                    pass_half(p, 0, f, True)
                with act.Fori(1, NC) as c:
                    for f in range(2):
                        pass_half(p, c, f, False)

        @block.vector
        def _(dve):
            dve.sem_inc(drained_v, 3)
            dve.sem_inc(cmp_v, 1)
            dve.sem_inc(z_used, 1)
            dve.sem_inc(zz_used, 1)
            dve.sem_inc(row_out, 1)
            k = Count(0)
            dve.wait_ge(w0_in, 48)
            for i in range(2):
                dve.tensor_tensor(wtmp[:, i, :], wcat[:, 16:], att[:, i, :], ALU.mult).then_inc(dve_step, k.up())
            dve.wait_ge(dve_step, k.now())
            for i in range(2):
                dve.tensor_reduce(wcat[:, i * H:(i + 1) * H],
                                  wtmp[:, i, :].rearrange("f (h d) -> f h d", h=H),
                                  AX.X, ALU.add).then_inc(watt_ready, 1)
            for k8 in range(1, NB, 2):
                dve.wait_ge(first_ready, k8 + 1)
                got = first[k8 % 4]
                dve.tensor_copy(feats[:, k8, :, :, :],
                                got[:, :, 16:16 + D].rearrange("p t (g c) -> p g t c", g=NG)
                                ).then_inc(first_v, 1)
                dve.tensor_copy(s_self[:, k8 * 8:(k8 + 1) * 8, :], got[:, :, 0:H]).then_inc(first_v, 1)
                dve.tensor_copy(s_neigh[:, :, k8 * 8:(k8 + 1) * 8, :],
                                got[:, :, H:2 * H].rearrange("p t (g h) -> p g t h", g=NG)
                                ).then_inc(first_v, 1)
            dve.wait_ge(first_v, 3 * NB // 2)
            dve.wait_ge(first_s, 3 * NB // 2)
            dve.tensor_reduce(nmax[:].rearrange("p (g h) -> p g h", g=NG),
                              s_neigh.rearrange("p g t h -> p g h t"), AX.X, ALU.max
                              ).then_inc(nmax_ready, 1)
            dve.tensor_scalar(nthr[:], s_neigh, -1.0, None, ALU.mult).then_inc(dve_step, k.up())
            dve.tensor_scalar(nbig[:], s_neigh, BIG, None, ALU.mult).then_inc(dve_step, k.up())
            dve.wait_ge(params, 16 * n_small)
            dve.tensor_copy(ident[:], identf[:]).then_inc(consts_ready, 1)
            dve.tensor_scalar(rx[:], rx[:], 1.0 / VS, None, ALU.mult).then_inc(consts_ready, 1)
            dve.tensor_scalar(wa[:], wa[:], 1.0 / VS, None, ALU.mult).then_inc(consts_ready, 1)
            dve.tensor_scalar(wb[:], wb[:], 1.0 / VS, None, ALU.mult).then_inc(consts_ready, 1)
            dve.tensor_scalar(sel2[:], sel2[:], 1.0 / VS, None, ALU.mult).then_inc(consts_ready, 1)
            for i in range(2):
                dve.tensor_tensor(gb[:, i, D:3 * D], gb[:, i, D:3 * D], gb2[:, i, :], ALU.add
                                  ).then_inc(consts_ready, 1)
            dve.wait_ge(nall_ready, 1)
            nall_g = nall[:].rearrange("p (g h) -> p g h", g=NG)
            dve.tensor_tensor(dd, s_neigh, nall_g.unsqueeze(2).to_broadcast([P, NG, T, GH]),
                              ALU.subtract).then_inc(dd_ready, 1)
            bn4 = bn[:].rearrange("p (c g) m h -> p g c m h", g=NG)
            ns4 = s_self.rearrange("p (c m) (g h) -> p g c m h", m=CT, g=NG)
            for g in range(NG):
                dve.tensor_tensor(bn4[:, g], ns4[:, g],
                                  nall_g[:, g].unsqueeze(1).unsqueeze(1).to_broadcast([P, NC, CT, GH]),
                                  ALU.add).then_inc(dve_step, k.up())
            dve.wait_ge(dve_step, k.now())
            dve.tensor_scalar(bn[:], bn[:], 0.0, None, ALU.max).then_inc(relu_ready, 1)
            dve.wait_ge(ry_ready, 1)
            dve.tensor_scalar(ry[:].rearrange("p k w -> p (k w)"), ps[:, 0, 0:384], 1.0 / VS, None, ALU.mult
                              ).then_inc(consts_ready, 1)
            dve.wait_ge(exps_ready, 4)
            with dve.Fori(0, NB // 2) as b2:
                kb = Count(b2 * (2 * K_BLOCK) + k.n)
                for i in range(2):
                    b = b2 * 2 + i
                    v4 = v18[i].rearrange("p (g x w) -> p g x w", g=NG, w=2 * VC)
                    dve.wait_ge(cast_done, b2 * 6 + (5 + i))
                    f4 = obuf[:].rearrange("p (b g x d) -> p b g x d", b=NB, g=NG, d=DH)[:, b]
                    for half, e in enumerate((fac0, fac1)):
                        eb = e.rearrange("p g (b t) h -> p b g (t h)", b=NB)[:, b].unsqueeze(3)
                        lo = half * VC
                        dve.tensor_tensor(v4[:, :, :, lo:lo + DH], f4,
                                          eb.to_broadcast([P, NG, BT * GH, DH]), ALU.mult
                                          ).then_inc(dve_step, kb.up())
                        last = dve.tensor_scalar(v4[:, :, :, lo + DH:lo + VC], eb, 1.0, None, ALU.mult)
                        if half == 0:
                            last.then_inc(dve_step, kb.up())
                    last.then_inc(rest_ready, 1)
                for s in range(SPLIT - 1):
                    for i in range(2):
                        dve.wait_ge(dve_step, kb.now())
                        dve.wait_ge(rest_ready, b2 * 6 + (s * 2 + i + 1))
                        dve.wait_ge(cast_done, b2 * 6 + (s * 2 + i + 7))
                        v3 = v18[i].rearrange("p (x k) -> p x k", k=VC)
                        dve.tensor_tensor(v3, v3, wst_parts[i][:, :, s * VC:(s + 1) * VC], ALU.subtract
                                          ).then_inc(rest_ready, 1)
                assert kb.n == 2 * K_BLOCK, kb.n
            k.n += NB * K_BLOCK
            for i in range(2):
                dve.wait_ge(w_stored[i], 16 + 8 * NB)

            def per_row(a, tiles=HT):
                return a.unsqueeze(2).to_broadcast([P, tiles, D])

            def post(it, g, kp):
                dve.wait_ge(z_ready, it + 2)
                dve.wait_ge(dve_step, kp.now())
                masked_sums = z0[:, :, 0:2 * GH * VC].rearrange("p m (h k) -> p m h k", h=GH)
                all_sums = z0[:, :, 2 * GH * VC:3 * GH * VC].rearrange("p m (h k) -> p m h k", h=GH)
                dve.tensor_copy(t1[:], all_sums).then_inc(dve_step, kp.up())
                dve.tensor_scalar(rdeg[:, it, :], z0[:, :, 3 * GH * VC], 1.0, None, ALU.add
                                  ).then_inc(dve_step, kp.up())
                dve.wait_ge(dve_step, kp.now())
                dve.tensor_tensor(t1[:], t1[:], masked_sums[:, :, :, VC:2 * VC], ALU.subtract
                                  ).then_inc(dve_step, kp.up())
                dve.wait_ge(dve_step, kp.now())
                dve.wait_ge(bn_ready, 1)
                dve.tensor_tensor(t1[:], t1[:], bn[:, it, :, :].unsqueeze(3).to_broadcast([P, CT, GH, VC]),
                                  ALU.mult).then_inc(dve_step, kp.up())
                dve.wait_ge(dve_step, kp.now())
                dve.tensor_tensor(t1[:], t1[:], masked_sums[:, :, :, 0:VC], ALU.add).then_inc(z_used, 1)
                dve.wait_ge(z_used, it + 2)
                dve.reciprocal(rden[:], t1[:, :, :, DH]).then_inc(dve_step, kp.up())
                dve.wait_ge(dve_step, kp.now())
                dve.tensor_tensor(o_now[:, g, :, :].rearrange("p m (h d) -> p m h d", h=GH),
                                  t1[:, :, :, 0:DH], rden[:].unsqueeze(3).to_broadcast([P, CT, GH, DH]),
                                  ALU.mult).then_inc(dve_step, kp.up())

            def norm_step(i, kk, u, q, st, tiles, dst):
                total, var, seed, half, y = (st[:, i, :] for i in range(5))
                dve.wait_ge(dve_step, kk.now())
                if i == 0:
                    op = dve.tensor_reduce(total, u, AX.X, ALU.add)
                elif i == 1:
                    op = dve.scalar_tensor_tensor(out=u, in0=per_row(total, tiles), scalar=-1.0 / D, in1=u,
                                                  op0=ALU.mult, op1=ALU.add)
                elif i == 2:
                    op = dve.tensor_tensor(q, u, u, ALU.mult)
                elif i == 3:
                    op = dve.tensor_reduce(var, q, AX.X, ALU.add)
                elif i == 4:
                    op = dve.tensor_scalar(var, var, 1.0 / D, EPS, ALU.mult, ALU.add)
                elif i == 5:
                    dve.tensor_scalar(half, var, -0.5, None, ALU.mult).then_inc(dve_step, kk.up())
                    op = dve.tensor_scalar(seed.bitcast(I32), var.bitcast(I32), 1, None,
                                           ALU.logical_shift_right)
                elif i == 6:
                    op = dve.tensor_scalar(y.bitcast(I32), seed.bitcast(I32), -1.0, float(0x5f3759df),
                                           ALU.mult, ALU.add)
                elif i == NORM_STEPS:
                    op = dve.tensor_tensor(dst, u, per_row(y, tiles), ALU.mult)
                elif i % 3 == 1:
                    op = dve.tensor_tensor(seed, y, y, ALU.mult)
                elif i % 3 == 2:
                    op = dve.tensor_tensor(seed, seed, half, ALU.mult)
                else:
                    op = dve.scalar_tensor_tensor(out=y, in0=seed, scalar=1.5, in1=y, op0=ALU.add, op1=ALU.mult)
                op.then_inc(dve_step, kk.up())

            def split_step(i, kk, src, dst):
                high, low = dst[:, :, 0:D], dst[:, :, D:2 * D]
                dve.wait_ge(dve_step, kk.now())
                if i == 0:
                    dve.tensor_scalar(high, src, VS, None, ALU.mult).then_inc(dve_step, kk.up())
                else:
                    dve.scalar_tensor_tensor(out=low, in0=src, scalar=VS, in1=high, op0=ALU.mult,
                                             op1=ALU.subtract).then_inc(v_ready, 1)

            def first_norm_step(i, c, kk):
                x_own = x_ch[:, c, :, :]
                if i == 0:
                    for g in range(NG):
                        dve.wait_ge(dve_step, kk.now())
                        dve.tensor_tensor(u_ch[:, :, g * 32:(g + 1) * 32], o_now[:, g, :, :],
                                          b0[:, g * 32:(g + 1) * 32].unsqueeze(1).to_broadcast([P, CT, 32]),
                                          ALU.add).then_inc(dve_step, kk.up())
                elif i == 1:
                    dve.wait_ge(dve_step, kk.now())
                    dve.wait_ge(x_in, 16)
                    dve.scalar_tensor_tensor(out=u_ch[:], in0=u_ch[:], scalar=0.0, in1=x_own, op0=ALU.max,
                                             op1=ALU.add).then_inc(dve_step, kk.up())
                elif i < 3 + NORM_STEPS:
                    norm_step(i - 2, kk, u_ch[:], q_ch[:], st_ch[:], CT, x_own)
                else:
                    split_step(i - 3 - NORM_STEPS, kk, x_own, vals_ch[:, c, :, :])

            def drain(it):
                dve.wait_ge(tiles_done, it * T + (CREDIT + T))
                dve.wait_ge(z_ready, it + 1)
                for bank in (0, 2, 4):
                    dve.tensor_copy(drained[:, bank, :], ps[:, bank, :]).then_inc(drained_v, 1)

            def attention_step(c, g, kk, behind, norm_behind):
                it = c * NG + g
                made_v, made_s = [0], [0]
                for jt in range(T + 1):
                    if jt < T:
                        dve.wait_ge(tiles_done, it * T + slot_free(jt))
                        if jt == 0:
                            dve.wait_ge(s_loaded[g], c * 16 + 16)
                        for h in dve_heads(jt):
                            dve.tensor_scalar(masks[:, jt % RING, h, :, :].rearrange("p f k -> p (f k)"),
                                              srow[g][:, h, :], nthr[:, g, jt, h:h + 1], ONE8, ALU.is_gt,
                                              ALU.mult).then_inc(cmp_v, 1)
                        made_v.append(made_v[-1] + len(dve_heads(jt)))
                        made_s.append(made_s[-1] + GH - len(dve_heads(jt)))
                    if behind and jt == 0:
                        drain(it - 1)
                    if jt > 0:
                        j = jt - 1
                        b, t = j // BT, j % BT
                        if t == 0:
                            dve.wait_ge(a_loaded[b], c * 16 + 16)
                        dve.wait_ge(cmp_v, it * V_CMP + (1 + made_v[jt]))
                        dve.wait_ge(cmp_s, it * S_CMP + (1 + made_s[jt]))
                        m = masks16[:, j % RING, :, :, :]
                        dve.tensor_tensor(m, m, a16[:, b, :, t, :].unsqueeze(1).to_broadcast(
                            [P, GH, 2, HALF // 2]), ALU.bitwise_and).then_inc(masked, 1)
                    if behind and jt == 8:
                        post(it - 1, 1 - g, kk)
                    if norm_behind and jt >= 12 and (jt - 12) // 2 < 5 + NORM_STEPS and jt % 2 == 0:
                        first_norm_step((jt - 12) // 2, c - 1, kk)

            kk = Count(k.n)
            attention_step(0, 0, kk, False, False)
            attention_step(0, 1, kk, True, False)
            assert kk.now() == k.n + K_POST, kk.n
            k0 = kk.now()
            with dve.Fori(1, NC) as c:
                kk = Count((c - 1) * (2 * K_POST + K_FIRST) + k0)
                attention_step(c, 0, kk, True, True)
                attention_step(c, 1, kk, True, False)
                assert kk.n == 2 * K_POST + K_FIRST, kk.n
            kk = Count(k0 + (NC - 1) * (2 * K_POST + K_FIRST))
            drain(IT - 1)
            post(IT - 1, 1, kk)
            for i in range(5 + NORM_STEPS):
                first_norm_step(i, NC - 1, kk)
            dve.wait_ge(cmp_s, IT * S_CMP + 1)
            dve.wait_ge(dve_step, kk.now())
            dve.reciprocal(rdeg[:], rdeg[:]).then_inc(dve_step, kk.up())
            k0 = kk.now()

            def norm(kk, dst):
                for i in range(NORM_STEPS + 1):
                    norm_step(i, kk, u, q, st, HT, dst)

            def split(kk, src, dst):
                for i in range(2):
                    split_step(i, kk, src, dst)

            def epilogue(p, c, f, k0):
                hf = c * 2 + f
                n = c * 2 + ((p - 1) * NH + f)
                kk = Count(c * (2 * K_PASS[p]) + (f * K_PASS[p] + k0))
                z = zz[f]
                if p < 4:
                    dve.wait_ge(v_ready, n + NC)
                else:
                    dve.wait_ge(row_out, c * 2 + (f + 1))
                dve.wait_ge(dve_step, kk.now())
                dve.wait_ge(zz_ready, n + 1)
                x_own = x_hf[:, hf, :, :]
                if p == 1:
                    dot = st[:, 5, :]
                    dve.tensor_tensor(q, z[:, :, 0:D], x_own, ALU.mult).then_inc(zz_used, 1)
                    dve.wait_ge(zz_used, n + 2)
                    dve.tensor_reduce(dot, q, AX.X, ALU.add).then_inc(dve_step, kk.up())
                    dve.scalar_tensor_tensor(out=u, in0=x_own, scalar=-0.1, in1=x_own, op0=ALU.mult, op1=ALU.add
                                             ).then_inc(dve_step, kk.up())
                    dve.wait_ge(dve_step, kk.now())
                    dve.tensor_scalar(dot, dot, -0.01, 1.0, ALU.mult, ALU.add).then_inc(dve_step, kk.up())
                    dve.wait_ge(dve_step, kk.now())
                    dve.tensor_tensor(u, u, per_row(dot), ALU.add).then_inc(dve_step, kk.up())
                    norm(kk, x_own)
                    split(kk, x_own, vals[1][:, hf, :, :])
                elif p < 4:
                    xin = x_own if p == 2 else h_hf[:, hf, :, :]
                    dve.tensor_tensor(gates, z, gb[:, p - 2, :].unsqueeze(1).to_broadcast([P, HT, GATES]),
                                      ALU.add).then_inc(zz_used, 1)
                    dve.wait_ge(gates_out, n - (NH - 1))
                    dve.tensor_tensor(nn[:], gates[:, :, D:2 * D], gates[:, :, 0:D], ALU.mult
                                      ).then_inc(dve_step, kk.up())
                    dve.wait_ge(dve_step, kk.now())
                    dve.tensor_tensor(nn[:], nn[:], gates[:, :, 3 * D:4 * D], ALU.add).then_inc(cand_in, 1)
                    dve.wait_ge(cand_out, n - (NH - 1))
                    dve.tensor_tensor(hh[:], xin, nn[:], ALU.subtract).then_inc(dve_step, kk.up())
                    dve.wait_ge(dve_step, kk.now())
                    dve.tensor_tensor(hh[:], hh[:], gates[:, :, 2 * D:3 * D], ALU.mult).then_inc(dve_step, kk.up())
                    dve.wait_ge(dve_step, kk.now())
                    dve.tensor_tensor(hh[:], hh[:], nn[:], ALU.add).then_inc(dve_step, kk.up())
                    dve.wait_ge(dve_step, kk.now())
                    if p == 2:
                        dve.tensor_scalar(h_hf[:, hf, :, :], hh[:], 0.0, None, ALU.max).then_inc(dve_step, kk.up())
                        split(kk, h_hf[:, hf, :, :], vals[0][:, hf, :, :])
                    else:
                        dve.scalar_tensor_tensor(out=u, in0=hh[:], scalar=0.0, in1=x_own, op0=ALU.max,
                                                 op1=ALU.add).then_inc(dve_step, kk.up())
                        norm(kk, x_own)
                        split(kk, x_own, vals[1][:, hf, :, :])
                else:
                    own = rdeg[:, c * 2, f * HT:(f + 1) * HT]
                    dve.tensor_tensor(u, z[:, :, D:2 * D], per_row(own), ALU.mult).then_inc(dve_step, kk.up())
                    dve.wait_ge(dve_step, kk.now())
                    dve.tensor_tensor(u, u, z[:, :, 0:D], ALU.add).then_inc(zz_used, 1)
                    dve.wait_ge(zz_used, n + 2)
                    dve.tensor_tensor(u, u, x_own, ALU.add).then_inc(dve_step, kk.up())
                    for i in range(NORM_STEPS):
                        norm_step(i, kk, u, q, st, HT, None)
                    dve.wait_ge(dve_step, kk.now())
                    dve.tensor_tensor(h_hf[:, hf, :, :], u, per_row(st[:, 4, :]), ALU.mult).then_inc(row_out, 1)
                assert kk.n == K_PASS[p], (p, kk.n)

            for p in range(1, 5):
                with dve.Fori(0, NC) as c:
                    for f in range(2):
                        epilogue(p, c, f, k0)
                k0 += NH * K_PASS[p]


_F32_INPUTS = ("adj", "xT", "xN", "W0", "attS", "attN", "bias0", "W1T", "wihT", "whhT", "bih", "bhh", "W3T",
               "consts")


def kernel(**inputs):
    import numpy as np
    import concourse.bacc as bacc
    from concourse.bass_utils import run_bass_kernel_spmd

    a = {k: np.asarray(v) for k, v in inputs.items()}

    add_pairs = np.zeros((P, 4 * VC), np.float32)
    add_all = np.zeros((P, GH * VC + 1), np.float32)
    for h in range(2):
        for s in range(SPLIT):
            for c in range(VC):
                e1_row, e2_row = (0, EW) if h == 0 else (HW + EW, HW)
                add_pairs[e1_row + s * VC + c, h * 2 * VC + c] = 1
                add_pairs[e2_row + s * VC + c, h * 2 * VC + VC + c] = 1
                for pair in range(2):
                    add_all[pair * HW + h * EW + s * VC + c, (pair * 2 + h) * VC + c] = 1
    add_all[ONES_AT - E2_AT, GH * VC] = 1
    eye = np.eye(P, dtype=np.float32)
    add_two = np.concatenate([eye[:D, :D], eye[:D, :D]])

    x, adj = a["x"], a["adj"]
    arrays = {
        "adj": np.ascontiguousarray(
            adj.reshape(NC, 2, HALF, NB, BT, P).transpose(0, 3, 5, 1, 4, 2)).reshape(NC, NB, P, -1),
        "xT": np.ascontiguousarray(x.T),
        "xN": np.ascontiguousarray(x.reshape(T, P, D).transpose(1, 0, 2)).reshape(P, T * D),
        "W0": a["L0_gnn_W"],
        "attS": a["L0_gnn_att_self"].reshape(D),
        "attN": a["L0_gnn_att_neigh"].reshape(D),
        "bias0": a["L0_gnn_bias"].reshape(D),
        "W1T": np.stack([a["L2_gnn_W1"].T, a["L2_gnn_W2"].T]),
        "wihT": np.stack([a["L2_gnn_wih1"].T, a["L2_gnn_wih2"].T]),
        "whhT": np.stack([a["L2_gnn_whh1"].T, a["L2_gnn_whh2"].T]),
        "bih": np.stack([a["L2_gnn_bih1"], a["L2_gnn_bih2"]]),
        "bhh": np.stack([a["L2_gnn_bhh1"], a["L2_gnn_bhh2"]]),
        "W3T": np.ascontiguousarray(a["L3_gnn_W"].T),
        "consts": np.concatenate([eye, add_pairs, add_all, add_two], axis=1),
    }
    nc = bacc.Bacc("TRN2", target_bir_lowering=False, num_devices=1)
    sent = {f"in_{k}": np.ascontiguousarray(arrays[k]) for k in _F32_INPUTS}
    aps = [nc.dram_tensor(k, v.shape, F32, kind="ExternalInput").ap() for k, v in sent.items()]
    out = nc.dram_tensor("out", (P, NH, HT * D), F32, kind="ExternalOutput").ap()
    build(nc, *aps, out)
    r = run_bass_kernel_spmd(nc, [sent], core_ids=[0])
    return np.ascontiguousarray(
        r.results[0]["out"].reshape(P, T, D).transpose(1, 0, 2)).reshape(N, D)
```

```python
from contextlib import ExitStack

import concourse.bass as bass
from concourse import mybir

F32, BF16, F16 = mybir.dt.float32, mybir.dt.bfloat16, mybir.dt.float16
F8, U8, U16, I32, U32 = (mybir.dt.float8e4, mybir.dt.uint8, mybir.dt.uint16, mybir.dt.int32,
                         mybir.dt.uint32)
ALU = mybir.AluOpType
ACT = mybir.ActivationFunctionType
AX = mybir.AxisListType

P = 128
N, D, H = 8192, 64, 8
DH = D // H
T = N // P
CH, HALF = 1024, 512
NC = N // CH
NH = N // HALF
BT = 8
NB = T // BT
CT = CH // P
HT = HALF // P
NG, GH = 2, 4
IT = NC * NG
VC = DH + 1
SPLIT = 3
EW = 32
HW = 2 * EW
E2_AT = EW
ONES_AT = 2 * EW - 1
WC = GH * HW
RING = 6
WSLOTS = 4
CREDIT = 32
BIG = float(2 ** 40)
ONE8 = 56.0
VS = 4096.0
EPS = 1e-5
QT = T // 4
GATES = 256
BANKS = 6


def dve_heads(g, jt):
    return [0] if jt % 4 == 3 and (jt != 3 if g == 0 else jt % 16 != 3 and jt % 32 != 27) else [0, 1]


def slot_free(jt):
    return CREDIT + (jt - RING if jt >= RING else (T - 1 - jt) // RING * RING + jt - T) + 1


def routed(jt):
    return jt >= ROUTE_FROM and jt % 2 == 0


ROUTE_FROM = 12
LEAD = 4
ROUTES = sum(routed(j) for j in range(T))

K_BLOCK, K_POST, K_FIRST = 3, 6, 22
K_PASS = {1: 23, 2: 6, 3: 24, 4: 19}
NORM_STEPS = 16

V_CMP = [sum(len(dve_heads(g, j)) for j in range(T)) for g in range(NG)]
S_CMP = [GH * T - v for v in V_CMP]


def cmp_v_at(c, g, jt):
    return c * sum(V_CMP) + (sum(V_CMP[:g]) + 1 + sum(len(dve_heads(g, j)) for j in range(jt + 1)))


def cmp_s_at(c, g, jt, but=0):
    return c * sum(S_CMP) + (sum(S_CMP[:g]) + 1 + sum(GH - len(dve_heads(g, j)) for j in range(jt + 1)) - but)


class Count:

    def __init__(self, base):
        self.base, self.n = base, 0

    def up(self):
        self.n += 1
        return 1

    def now(self):
        return self.base + self.n


def build(nc, adj, xT, xN, W0, attS, attN, bias0, W1T, wihT, whhT, bih, bhh, W3T, consts, out):
    with ExitStack() as ctx:
        def sb(name, shape, dt):
            return ctx.enter_context(nc.sbuf_tensor(name, shape, dt))

        def sem(name):
            return ctx.enter_context(nc.semaphore(name))

        adj8 = nc.dram_tensor("adj8", (NH, 4, P, 2, BT * HALF), U8, kind="Internal").ap()
        w_tab = nc.dram_tensor("w_tab", (NG, NB, P, BT * WC), BF16, kind="Internal").ap()
        s_parts = nc.dram_tensor("s_parts", (SPLIT + 1, NG, NC, CH), BF16, kind="Internal").ap()
        s_rows = nc.dram_tensor("s_rows", (NC, H, CH), F32, kind="Internal").ap()

        abuf = sb("abuf", [P, NB, 2, BT, HALF], U8)
        a8 = abuf[:].bitcast(F8)
        a16 = abuf[:].bitcast(U16)
        wring = sb("wring", [P, WSLOTS, BT, WC], BF16)
        early = sb("early", [P, GH * CH * 4 + RING * GH * CH], U8)
        masks = early[:, GH * CH * 4:].rearrange("p (s h f k) -> p s h f k", s=RING, h=GH, f=2)
        masks8 = masks.bitcast(F8)
        masks16 = masks.bitcast(U16)
        VB = T * P * 2
        vals0 = sb("vals0", [P, T * P], F16)
        vals = [v.rearrange("p (f m k) -> p f m k", f=NH, m=HT)
                for v in (vals0[:], early[:, 0:VB].bitcast(F16))]
        vals_ch = vals0[:].rearrange("p (c m k) -> p c m k", c=NC, m=CT)
        stage_at = GH * CH * 4
        WST = NG * BT * WC * 2
        wst = [early[:, stage_at + i * WST:stage_at + (i + 1) * WST].bitcast(BF16) for i in range(2)]
        wst += [vals0[:, i * WST // 2:(i + 1) * WST // 2].bitcast(BF16) for i in range(2)]
        wst_parts = [w.rearrange("p (x e) -> p x e", e=EW) for w in wst]
        gbuf = sb("gbuf", [P, BANKS * HALF * 4], U8)
        drained = gbuf[:].bitcast(F32).rearrange("p (b k) -> p b k", b=BANKS)
        VBLOCK = BT * H * 2 * VC
        v18 = [gbuf[:, i * VBLOCK * 4:(i + 1) * VBLOCK * 4].bitcast(F32) for i in range(2)]
        ybuf = [drained[:, i, :] for i in range(2)]
        xt_sb = drained[:, 2, :]
        gates = gbuf[:, 3 * 2048:5 * 2048].bitcast(F32).rearrange("p (m k) -> p m k", m=HT)
        xbuf = sb("xbuf", [P, T * D], F32)
        x_hf = xbuf[:].rearrange("p (f m d) -> p f m d", f=NH, m=HT)
        x_ch = xbuf[:].rearrange("p (c m d) -> p c m d", c=NC, m=CT)
        s_self = xbuf[:, 0:512].rearrange("p (t h) -> p t h", t=T)
        s_neigh, dd, fac0, fac1 = (xbuf[:, 512 * i:512 * (i + 1)].rearrange("p (g t h) -> p g t h", g=NG, t=T)
                                   for i in range(1, 5))
        obuf = sb("obuf", [P, T * D], F32)
        feats = obuf[:].rearrange("p (b g t c) -> p b g t c", b=NB, g=NG, t=BT)
        h_hf = obuf[:].rearrange("p (f m d) -> p f m d", f=NH, m=HT)
        srow = [a.rearrange("p (h r) -> p h r", h=GH) for a in (early[:, 0:GH * CH * 4].bitcast(F32), obuf[:])]
        o_now = sb("o_now", [P, NG, CT, GH * DH], F32)
        xT_sb = abuf[0:D, NB // 2:, :, :, :].rearrange("p a b c d -> p (a b c d)").bitcast(F32)
        srowT = gbuf[:, 9216:9216 + 2048].bitcast(F32).rearrange("p (q k) -> p q k", q=4)
        bn = sb("bn", [P, IT, CT, GH], F32)
        nthr = sb("nthr", [P, NG, T, GH], F32)
        nbig = sb("nbig", [P, NG, T, GH], F32)
        rdeg = sb("rdeg", [P, IT, CT], F32)
        t1 = sb("t1", [P, CT, GH, VC], F32)
        rden = sb("rden", [P, CT, GH], F32)
        u_ch = sb("u", [P, CT, D], F32)
        q_ch = sb("q", [P, CT, D], F32)
        st_ch = sb("st", [P, 6, CT], F32)
        u, q, st = u_ch[:, 0:HT, :], q_ch[:, 0:HT, :], st_ch[:, :, 0:HT]
        nnhh = sb("nnhh", [P, 2, HT, D], F32)
        nn, hh = nnhh[:, 0, :, :], nnhh[:, 1, :, :]
        hsrc = q_ch[:].rearrange("p m d -> p (m d)")[:, 0:P]
        hparts = u_ch[:].bitcast(BF16).rearrange("p m d -> p (m d)")[:, 0:(SPLIT + 1) * P].rearrange(
            "p (s k) -> p s k", k=P)
        lmax = sb("lmax", [P, 2], F32)
        l16 = sb("l16", [P, 2], BF16)
        diagL = sb("diagL", [P, P], BF16)
        rowL = sb("rowL", [SPLIT + 1, P], BF16)
        wcat = sb("wcat", [D, 16 + D], F32)
        att, wtmp = nn[0:D, 0:2, :], hh[0:D, 0:2, :]
        b0 = sb("b0", [P, D], F32)
        selP = sb("selP", [P, 2 * 2 * VC], F32)
        selA = sb("selA", [P, GH * VC + 1], F32)
        sel2 = sb("sel2", [P, D], F32)
        identf = sb("identf", [P, P], F32)
        ident = sb("ident", [P, P], F16)
        nmax = sb("nmax", [P, H + 1], F32)
        nall = sb("nall", [P, H + 1], F32)
        wbuf = sb("wbuf", [D, 4 * D + 6 * D], F32)
        w1t = wbuf[:, 0:4 * D].rearrange("p (k r d) -> p k r d", k=2, r=2)
        wih = wbuf[:, 4 * D:].rearrange("p (k d) -> p k d", k=2)
        srt = [nnhh[0:SPLIT + 1].rearrange("p a m d -> p (a m d)").bitcast(BF16),
               wbuf[0:SPLIT + 1, 0:CH // 2].bitcast(BF16)]
        rx = sb("rx", [P, 2, 3 * D], F32)
        ry = sb("ry", [P, 2, 3 * D], F32)
        gb = sb("gb", [P, 2, GATES], F32)
        gb2 = sb("gb2", [P, 2, 2 * D], F32)
        wa = sb("wa", [P, D], F32)
        wb = sb("wb", [P, D], F32)

        ps = ctx.enter_context(nc.psum_tensor("ps", [P, 8, HALF], F32))
        first = [ps[:, 2 * i:2 * i + 2, :].rearrange("p b (t k) -> p (b t) k", k=P) for i in range(4)]
        z0 = ps[:, 6:8, :].rearrange("p b (m k) -> p (b m) k", m=4)
        zz = [ps[:, 4 + 2 * i:6 + 2 * i, :].rearrange("p b (m k) -> p (b m) k", m=2) for i in range(2)]

        params = sem("params")
        w0_in = sem("w0_in")
        xT_in = [sem(f"xT_in{i}") for i in range(4)]
        x_in = sem("x_in")
        watt_ready = sem("watt_ready")
        first_ready = sem("first_ready")
        first_v = sem("first_v")
        first_s = sem("first_s")
        turned = sem("turned")
        turned_out = sem("turned_out")
        rows_stored = sem("rows_stored")
        nmax_ready = sem("nmax_ready")
        nall_ready = sem("nall_ready")
        dd_ready = sem("dd_ready")
        exps_ready = sem("exps_ready")
        relu_ready = sem("relu_ready")
        bn_ready = sem("bn_ready")
        zeroed = sem("zeroed")
        cast_done = sem("cast_done")
        rest_ready = sem("rest_ready")
        w_stored = [sem(f"w_stored{i}") for i in range(4)]
        dve_step = sem("dve_step")
        a_loaded = [sem(f"a_loaded{b}") for b in range(NB)]
        a_stored = [sem(f"a_stored{b}") for b in range(NB)]
        w_loaded = [sem(f"w_loaded{k}") for k in range(WSLOTS)]
        s_loaded = [sem(f"s_loaded{g}") for g in range(NG)]
        hs_in = sem("hs_in")
        hs_split = sem("hs_split")
        parts_stored = sem("parts_stored")
        L_ready = sem("L_ready")
        parts_loaded = [sem(f"parts_loaded{g}") for g in range(NG)]
        route_ready = sem("route_ready")
        cmp_v = sem("cmp_v")
        cmp_s = sem("cmp_s")
        masked = sem("masked")
        tiles_done = sem("tiles_done")
        drained_s = sem("drained_s")
        z_ready = sem("z_ready")
        z_used = sem("z_used")
        gate = sem("gate")
        ry_ready = sem("ry_ready")
        consts_ready = sem("consts_ready")
        v_ready = sem("v_ready")
        q_loaded = [sem(f"q_loaded{k}") for k in range(8)]
        q_done = sem("q_done")
        y_out = sem("y_out")
        xt_ready = sem("xt_ready")
        xt_out = sem("xt_out")
        xz_done = sem("xz_done")
        zz_ready = sem("zz_ready")
        zz_used = sem("zz_used")
        gates_out = sem("gates_out")
        cand_in = sem("cand_in")
        cand_out = sem("cand_out")
        row_out = sem("row_out")
        stored = sem("stored")

        block = ctx.enter_context(nc.Block())

        def lead(eng):
            eng.sem_inc(gate, 1)

        n_small = 5 + 2 * (1 + 6 + 4) + 4

        @block.sync
        def _(sp):
            def small(dst, src):
                sp.dma_start(dst, src).then_inc(params, 16)

            sp.dma_start(wcat[:, 16:], W0).then_inc(w0_in, 16)
            sp.dma_start(att[:, 0, :], attS.partition_broadcast(D)).then_inc(w0_in, 16)
            sp.dma_start(att[:, 1, :], attN.partition_broadcast(D)).then_inc(w0_in, 16)
            for i in range(4):
                cols = slice(i * (N // 4), (i + 1) * (N // 4))
                sp.dma_start(xT_sb[:, cols], xT[:, cols]).then_inc(xT_in[i], 16)
            small(b0[:], bias0.partition_broadcast(P))
            small(identf[:], consts[:, 0:P])
            small(selP[:], consts[:, P:P + 36])
            small(selA[:], consts[:, P + 36:P + 73])
            small(sel2[:], consts[:, P + 73:P + 73 + D])
            for k in range(2):
                small(wih[:, k, :], wihT[k])
                for r in range(2):
                    small(w1t[:, k, r, :], W1T[k])
                    small(rx[r * D:(r + 1) * D, k, D:3 * D], whhT[k][:, 0:2 * D])
                    small(rx[r * D:(r + 1) * D, k, 0:D], whhT[k][:, 2 * D:3 * D])
                small(gb[:, k, D:3 * D], bih[k, 0:2 * D].partition_broadcast(P))
                small(gb2[:, k, :], bhh[k, 0:2 * D].partition_broadcast(P))
                small(gb[:, k, 0:D], bhh[k, 2 * D:3 * D].partition_broadcast(P))
                small(gb[:, k, 3 * D:4 * D], bih[k, 2 * D:3 * D].partition_broadcast(P))
            for r in range(2):
                small(wa[r * D:(r + 1) * D, :], W3T[0:D, :])
                small(wb[r * D:(r + 1) * D, :], W3T[D:2 * D, :])
            for k in range(4):
                sp.wait_ge(turned_out, k + 1)
                lead(sp)
                for c in range(2):
                    sp.dma_start(s_rows[2 * k + c].rearrange("h (m p) -> m h p", p=P),
                                 srowT[c * D:(c + 1) * D, k, :]).then_inc(rows_stored, 16)
            def load_rows(c, g):
                sp.dma_start(srow[g], s_rows[c, g * GH:(g + 1) * GH, :].partition_broadcast(P)
                             ).then_inc(s_loaded[g], 16)

            def load_parts(c, g):
                sp.dma_start(srt[g], s_parts[:, g, c, :]).then_inc(parts_loaded[g], 16)

            sp.wait_ge(rows_stored, 16 * 8)
            load_rows(0, 0)
            for g in range(NG):
                sp.dma_start(hsrc[g * D:(g + 1) * D, :],
                             s_rows[:, g * GH + GH - 1, :].rearrange("c (m k) -> c m k", m=CT)
                             ).then_inc(hs_in, 16)
            with sp.Fori(0, NB // 4) as k:
                for w in range(4):
                    sp.wait_ge(cast_done, k * 12 + (w // 2 * 6 + w % 2 + 11))
                    lead(sp)
                    sp.dma_start(w_tab[:, k * 4 + w, :, :].rearrange("g p w -> p g w"),
                                 wst[w].rearrange("p (g w) -> p g w", g=NG)).then_inc(w_stored[w], 16)
            sp.wait_ge(hs_split, 6)
            sp.dma_start(s_parts.rearrange("s g c (m k) -> (g c m) s k", m=CT), hparts
                         ).then_inc(parts_stored, 16)
            for w in range(4):
                sp.wait_ge(w_stored[w], 16 + 4 * NB)
            sp.wait_ge(ry_ready, 1)
            sp.wait_ge(parts_stored, 16)
            load_parts(0, 0)

            def chunk_loads(c, last):
                for g in range(NG):
                    for b in range(NB):
                        sp.wait_ge(tiles_done,
                                   c * (NG * T) + (g * T + CREDIT + (b - WSLOTS + 1) * BT))
                        lead(sp)
                        sp.dma_start(wring[:, b % WSLOTS, :, :].rearrange("p t w -> p (t w)"),
                                     w_tab[g, b, :, :]).then_inc(w_loaded[b % WSLOTS], 16)
                        if g == 1 and b == 0:
                            load_rows(c, 1)
                            load_parts(c, 1)
                        if g == 1 and b == WSLOTS and not last:
                            load_rows(c + 1, 0)
                            load_parts(c + 1, 0)
                        if g == 0:
                            sp.wait_ge(a_loaded[b], c * 16 + 16)
                            lead(sp)
                            sp.dma_start(
                                adj8[bass.ds(c * 2, 2), b // 2, :, b % 2, :].rearrange("f p k -> p f k"),
                                abuf[:, b, :, :, :].rearrange("p f t k -> p f (t k)")
                            ).then_inc(a_stored[b], 16)

            with sp.Fori(0, NC - 1) as c:
                chunk_loads(c, False)
            chunk_loads(NC - 1, True)
            def load_adj8(c, slot):
                sp.dma_start(abuf[:, slot, :, :, :].rearrange("p f t k -> p (f t k)"),
                             adj8[c * 2 + slot // 4, slot % 4, :, :, :].rearrange("p b k -> p (b k)")
                             ).then_inc(q_loaded[slot], 16)

            for b in range(NB):
                sp.wait_ge(a_stored[b], 16 * NC)
            for slot in range(8):
                sp.wait_ge(tiles_done, CREDIT + (IT - 1) * T + (slot + 1) * BT)
                load_adj8(0, slot)
            for p in range(4):
                with sp.Fori(1 if p == 0 else 0, NC) as c:
                    for slot in range(8):
                        sp.wait_ge(q_done, c * 8 + (p * 64 + slot + 1))
                        lead(sp)
                        load_adj8(c, slot)
            with sp.Fori(0, NH) as n:
                sp.wait_ge(row_out, n + 2)
                lead(sp)
                sp.dma_start(out[:, n, :], h_hf[:, n, :, :].rearrange("p m d -> p (m d)")
                             ).then_inc(stored, 16)
            sp.wait_ge(stored, 16 * NH)

        @block.gpsimd
        def _(pool):
            def load_adj(c, b):
                pool.dma_start(a8[:, b, :, :, :].rearrange("p f t k -> p (f t k)"),
                               adj[c, b, :, :]).then_inc(a_loaded[b], 16)

            for i in range(4):
                pool.memset(wst[i].bitcast(U32), 0).then_inc(zeroed, 1)
            pool.wait_ge(zeroed, 4)
            for i in range(4):
                pool.memset(wst[i].rearrange("p (x w) -> p x w", w=2 * HW)[:, :, ONES_AT:ONES_AT + 1], 1.0
                            ).then_inc(zeroed, 1)
            pool.memset(rowL[:], 1.0).then_inc(zeroed, 1)
            for i in range(4):
                pool.wait_ge(xT_in[i], 16)
            for b in range(NB // 2):
                load_adj(0, b)
            pool.wait_ge(nmax_ready, 2)
            pool.partition_all_reduce(nall[:], nmax[:], P, bass.bass_isa.ReduceOp.max).then_inc(nall_ready, 1)
            pool.wait_ge(first_ready, NB)
            for b in range(NB // 2, NB):
                load_adj(0, b)
            pool.wait_ge(rest_ready, 3 * NB)
            pool.wait_ge(tiles_done, CREDIT + BT)
            pool.dma_start(xbuf[:], xN).then_inc(x_in, 16)
            for c in range(1, NC):
                for b in range(NB):
                    pool.wait_ge(tiles_done, CREDIT + (2 * c - 1) * T + (b + 1) * BT)
                    pool.wait_ge(a_stored[b], 16 * c)
                    load_adj(c, b)

        @block.tensor
        def _(pe):
            pe.sem_inc(tiles_done, CREDIT)
            pe.sem_inc(z_ready, 1)
            pe.sem_inc(q_done, 8)
            pe.wait_ge(w0_in, 48)
            pe.wait_ge(watt_ready, 2)
            for k in range(NB):
                if k % 2 == 0:
                    pe.wait_ge(xT_in[k // 2], 16)
                if k >= 4:
                    pe.wait_ge((first_s, first_v)[k % 2], 3 * ((k - 4) // 2 + 1))
                for m in range(8):
                    mm = pe.matmul(first[k % 4][:, m, 0:16 + D],
                                   xT_sb[:, (k * 8 + m) * P:(k * 8 + m + 1) * P], wcat[:],
                                   start=True, stop=True)
                mm.then_inc(first_ready, 1)
            pe.wait_ge(first_s, 3 * NB // 2)
            pe.wait_ge(first_v, 3 * NB // 2)
            pe.wait_ge(params, 16 * n_small)
            for k in range(4):
                pe.matmul(ps[:, 2 + k, 0:P], xbuf[:, k * P:(k + 1) * P], identf[:],
                          start=True, stop=True).then_inc(turned, 1)
            for k in range(2):
                mm = pe.matmul(ps[:, 0, k * 192:(k + 1) * 192], w1t[:, k].rearrange("p r d -> p (r d)"),
                               wih[:, k, :], start=True, stop=True)
            mm.then_inc(ry_ready, 1)
            pe.wait_ge(turned_out, 4)
            pe.wait_ge(consts_ready, 1)

            def route(c, g, jt):
                it = c * NG + g
                b, t = jt // BT, jt % BT
                if jt == ROUTE_FROM:
                    pe.wait_ge(parts_loaded[g], c * 16 + 16)
                    pe.wait_ge(z_used, it + 1)
                else:
                    before = max(j for j in range(jt) if routed(j))
                    pe.wait_ge(cmp_s, cmp_s_at(c, g, before))
                lead(pe)
                if jt == ROUTE_FROM or before < b * BT:
                    pe.wait_ge(a_loaded[b], c * 16 + 16)
                    lead(pe)
                for f in range(2):
                    pe.matmul(ps[:, 6 + f, :], diagL[:], a8[:, b, f, t, :], start=True, stop=False)
                    mm = pe.matmul(ps[:, 6 + f, :], rowL[:], srt[g][:, f * HALF:(f + 1) * HALF],
                                   start=False, stop=True)
                mm.then_inc(route_ready, 1)

            def tile_sums(c, g, b, t):
                it = c * NG + g
                jt = b * BT + t
                ws = wring[:, b % WSLOTS, t, :]
                if t == 0:
                    pe.wait_ge(w_loaded[b % WSLOTS], it * 32 + (16 * (b // WSLOTS) + 16))
                    lead(pe)
                pe.wait_ge(masked, it * T + (jt + 1))
                lead(pe)
                if routed(jt):
                    pe.wait_ge(cmp_s, cmp_s_at(c, g, jt))
                    lead(pe)
                for f in range(2):
                    for h in range(GH):
                        r = (h % 2) * HW
                        pe.matmul(ps[r:r + HW, f * 3 + h // 2, :], ws[:, h * HW:(h + 1) * HW],
                                  masks8[:, jt % RING, h, f, :], start=(jt == 0), stop=(jt == T - 1),
                                  skip_group_check=True)
                    for pair in range(2):
                        r, at = pair * HW, pair * 2 * HW + E2_AT
                        mm = pe.matmul(ps[r:r + HW, f * 3 + 2, :], ws[:, at:at + HW], a8[:, b, f, t, :],
                                       start=(jt == 0), stop=(jt == T - 1), skip_group_check=True)
                mm.then_inc(tiles_done, 1)

            def gather(it):
                pe.wait_ge(drained_s, (it + 2) * BANKS)
                pe.wait_ge(z_used, it + 1)
                lead(pe)
                for f in range(2):
                    for m in range(HT):
                        for k in range(3):
                            w = GH * VC + 1 if k == 2 else 4 * VC
                            mm = pe.matmul(z0[:, f * HT + m, k * 36:k * 36 + w],
                                           drained[:, f * 3 + k, m * P:(m + 1) * P],
                                           (selA if k == 2 else selP)[:], start=True, stop=True)
                mm.then_inc(z_ready, 1)

            def attention_step(c, g, behind):
                it = c * NG + g
                pe.wait_ge(drained_s, (it + 1) * BANKS)
                lead(pe)
                for b in range(NB):
                    for t in range(BT):
                        if b * BT + t + LEAD < T and routed(b * BT + t + LEAD):
                            route(c, g, b * BT + t + LEAD)
                        tile_sums(c, g, b, t)
                        if behind and b == 0 and t == 3:
                            gather(it - 1)

            pe.wait_ge(L_ready, 4)
            attention_step(0, 0, False)
            attention_step(0, 1, True)
            with pe.Fori(1, NC) as c:
                for g in range(NG):
                    attention_step(c, g, True)
            gather(IT - 1)
            pe.wait_ge(consts_ready, 8)

            def x_part(p, n, f):
                pe.wait_ge(xt_out, n - (NH - 1))
                pe.wait_ge(zz_used, n)
                lead(pe)
                w, cols = (rx[:, p - 2, :], 3 * D) if p < 4 else (wa[:], D)
                for m in range(HT):
                    mm = pe.matmul(zz[f][:, m, 0:cols], xt_sb[:, m * P:(m + 1) * P], w,
                                   start=(m % 2 == 0), stop=True, skip_group_check=True)
                mm.then_inc(xz_done, 1)

            def y_part(p, n, f, first=False):
                pe.wait_ge(y_out, n + 1)
                if p == 1 and f == 1 and first:
                    pe.wait_ge(z_used, IT + 1)
                if p == 1 and not first:
                    pe.wait_ge(zz_used, n)
                lead(pe)
                for m in range(HT):
                    lhs = ybuf[f][:, m * P:(m + 1) * P]
                    if p == 1:
                        mm = pe.matmul(zz[f][:, m, 0:D], lhs, sel2[:], start=(m % 2 == 0), stop=True,
                                       skip_group_check=True)
                    elif p == 4:
                        mm = pe.matmul(zz[f][:, m, D:2 * D], lhs, wb[:], start=False, stop=True,
                                       skip_group_check=True)
                    else:
                        mm = pe.matmul(zz[f][:, m, D:4 * D], lhs, ry[:, p - 2, :], start=False, stop=True,
                                       skip_group_check=True)
                mm.then_inc(zz_ready, 1)

            def pass_half(p, c, f, behind):
                base = (p - 1) * NH
                n = c * 2 + (base + f)
                first = isinstance(c, int)
                v = vals[(p - 1) % 2]
                if not (first and n < 2):
                    pe.wait_ge(y_out, n - 1)
                    lead(pe)
                for jt in range(T):
                    slot = f * 4 + jt // QT
                    if jt % QT == 0:
                        pe.wait_ge(q_loaded[slot], c * 16 + ((p - 1) * NC * 16 + 16))
                        lead(pe)
                    if first and p == 1 and jt % CT == 0:
                        pe.wait_ge(v_ready, jt // CT + 1)
                    if first and p > 1 and jt % HT == 0:
                        pe.wait_ge(v_ready, NC + base - NH + jt // HT + 1)
                    mm = pe.matmul(ps[:, f, :], v[:, jt // HT, jt % HT, :],
                                   a8[:, slot, (jt % QT) // BT, jt % BT, :],
                                   start=(jt == 0), stop=(jt == T - 1))
                    if jt % QT == QT - 1:
                        mm.then_inc(q_done, 1)
                    if p > 1 and jt == 8:
                        if not (first and n == NH):
                            pe.wait_ge(xt_out, n - NH)
                            lead(pe)
                        for m in range(HT):
                            mm = pe.matmul(ps[:, 2, m * P:(m + 1) * P], v[:, c * 2 + f, m, :], ident[:],
                                           start=True, stop=True)
                        mm.then_inc(xt_ready, 1)
                    if behind and jt == 20:
                        y_part(p, n - 1, 1 - f, first and n == 1)
                    if p > 1 and jt == 56:
                        x_part(p, n, f)

            for p in range(1, 5):
                pass_half(p, 0, 0, False)
                pass_half(p, 0, 1, True)
                with pe.Fori(1, NC) as c:
                    pass_half(p, c, 0, True)
                    pass_half(p, c, 1, True)
                y_part(p, p * NH - 1, 1)

        @block.scalar
        def _(act):
            act.sem_inc(drained_s, BANKS)
            act.sem_inc(cmp_s, 1)
            for w in range(4):
                act.sem_inc(w_stored[w], 16)
            act.sem_inc(cast_done, 6)
            for k in range(0, NB, 2):
                act.wait_ge(first_ready, k + 1)
                got = first[k % 4]
                act.copy(feats[:, k, :, :, :], got[:, :, 16:16 + D].rearrange("p t (g c) -> p g t c", g=NG)
                         ).then_inc(first_s, 1)
                act.copy(s_self[:, k * 8:(k + 1) * 8, :], got[:, :, 0:H]).then_inc(first_s, 1)
                act.copy(s_neigh[:, :, k * 8:(k + 1) * 8, :],
                         got[:, :, H:2 * H].rearrange("p t (g h) -> p g t h", g=NG)).then_inc(first_s, 1)
            for k in range(4):
                act.wait_ge(turned, k + 1)
                act.copy(srowT[:, k, :], ps[:, 2 + k, 0:P]).then_inc(turned_out, 1)
            act.wait_ge(dd_ready, 1)
            def heads_of(a, odd):
                return a.rearrange("p g t (h two) -> p (g t h) two", two=2)[:, :, odd]

            for odd in range(2):
                act.activation(heads_of((fac0, fac1)[odd], odd), heads_of(dd, odd), ACT.Exp
                               ).then_inc(exps_ready, 1)
                act.activation(heads_of((fac1, fac0)[odd], odd), heads_of(dd, odd), ACT.Exp, scale=0.2
                               ).then_inc(exps_ready, 1)
            act.wait_ge(relu_ready, 1)
            act.activation(bn[:], bn[:], ACT.Exp, scale=-0.8).then_inc(bn_ready, 1)
            act.wait_ge(zeroed, 8)
            with act.Fori(0, NB // 4) as k:
                for pair in range(2):
                    for s in range(SPLIT):
                        for i in range(2):
                            w = pair * 2 + i
                            act.wait_ge(rest_ready, k * 12 + (pair * 6 + s * 2 + i + 1))
                            if s == 0:
                                act.wait_ge(w_stored[w], k * 16 + 16)
                            lead(act)
                            act.copy(wst_parts[w][:, :, s * VC:(s + 1) * VC],
                                     v18[i].rearrange("p (x k) -> p x k", k=VC)).then_inc(cast_done, 1)
            for w in range(2):
                act.wait_ge(w_stored[w], 16 + 4 * NB)

            def drain(it):
                act.wait_ge(tiles_done, it * T + (CREDIT + T))
                act.wait_ge(z_ready, it + 1)
                for k in range(BANKS):
                    act.copy(drained[:, k, :], ps[:, k, :]).then_inc(drained_s, 1)

            def attention_step(c, g, behind):
                it = c * NG + g
                act.wait_ge(s_loaded[g], c * 16 + 16)
                lead(act)
                for jt in range(T):
                    act.wait_ge(tiles_done, it * T + slot_free(jt))
                    lead(act)
                    for h in range(len(dve_heads(g, jt)), GH):
                        scores = srow[g][:, h, :]
                        if h == GH - 1 and routed(jt):
                            done = sum(routed(j) for j in range(jt))
                            act.wait_ge(route_ready, it * ROUTES + (done + 1))
                            lead(act)
                            scores = ps[:, 6:8, :].rearrange("p f k -> p (f k)")
                        act.activation(masks8[:, jt % RING, h, :, :].rearrange("p f k -> p (f k)"),
                                       scores, ACT.Sigmoid, bias=nbig[:, g, jt, h:h + 1],
                                       scale=BIG, saturate=False).then_inc(cmp_s, 1)
                    if behind and jt == 1:
                        drain(it - 1)

            attention_step(0, 0, False)
            attention_step(0, 1, True)
            with act.Fori(1, NC) as c:
                for g in range(NG):
                    attention_step(c, g, True)
            drain(IT - 1)
            act.wait_ge(z_used, IT + 1)

            def pass_half(p, c, f, first):
                n = c * 2 + ((p - 1) * NH + f)
                if p > 1:
                    act.wait_ge(xt_ready, n - (NH - 1))
                    if not (first and n == NH):
                        act.wait_ge(xz_done, n - NH)
                    act.copy(xt_sb, ps[:, 2, :]).then_inc(xt_out, 1)
                act.wait_ge(q_done, n * 4 + 12)
                if not (first and n < 2):
                    act.wait_ge(zz_ready, n - 1)
                act.copy(ybuf[f], ps[:, f, :]).then_inc(y_out, 1)
                if p in (2, 3):
                    act.wait_ge(zz_used, n + 2)
                    act.activation(gates[:, :, D:3 * D], gates[:, :, D:3 * D], ACT.Sigmoid
                                   ).then_inc(gates_out, 1)
                    act.wait_ge(cand_in, n - (NH - 1))
                    act.activation(nn[:], nn[:], ACT.Tanh).then_inc(cand_out, 1)

            for p in range(1, 5):
                for f in range(2):
                    pass_half(p, 0, f, True)
                with act.Fori(1, NC) as c:
                    for f in range(2):
                        pass_half(p, c, f, False)

        @block.vector
        def _(dve):
            dve.sem_inc(cmp_v, 1)
            dve.sem_inc(z_used, 1)
            dve.sem_inc(zz_used, 1)
            dve.sem_inc(row_out, 1)
            k = Count(0)
            dve.wait_ge(w0_in, 48)
            for i in range(2):
                dve.tensor_tensor(wtmp[:, i, :], wcat[:, 16:], att[:, i, :], ALU.mult).then_inc(dve_step, k.up())
            dve.wait_ge(dve_step, k.now())
            for i in range(2):
                dve.tensor_reduce(wcat[:, i * H:(i + 1) * H],
                                  wtmp[:, i, :].rearrange("f (h d) -> f h d", h=H),
                                  AX.X, ALU.add).then_inc(watt_ready, 1)
            for k8 in range(1, NB, 2):
                dve.wait_ge(first_ready, k8 + 1)
                got = first[k8 % 4]
                dve.tensor_copy(feats[:, k8, :, :, :],
                                got[:, :, 16:16 + D].rearrange("p t (g c) -> p g t c", g=NG)
                                ).then_inc(first_v, 1)
                dve.tensor_copy(s_self[:, k8 * 8:(k8 + 1) * 8, :], got[:, :, 0:H]).then_inc(first_v, 1)
                dve.tensor_copy(s_neigh[:, :, k8 * 8:(k8 + 1) * 8, :],
                                got[:, :, H:2 * H].rearrange("p t (g h) -> p g t h", g=NG)
                                ).then_inc(first_v, 1)
            dve.wait_ge(first_v, 3 * NB // 2)
            dve.wait_ge(first_s, 3 * NB // 2)
            dve.tensor_reduce(nmax[:, 0:H].rearrange("p (g h) -> p g h", g=NG),
                              s_neigh.rearrange("p g t h -> p g h t"), AX.X, ALU.max
                              ).then_inc(nmax_ready, 1)
            dve.tensor_reduce(nmax[:, H:H + 1], s_self.rearrange("p t h -> p (t h)"), AX.X, ALU.max
                              ).then_inc(nmax_ready, 1)
            dve.tensor_scalar(nthr[:], s_neigh, -1.0, None, ALU.mult).then_inc(dve_step, k.up())
            dve.tensor_scalar(nbig[:], s_neigh, BIG, None, ALU.mult).then_inc(dve_step, k.up())
            dve.wait_ge(params, 16 * n_small)
            dve.tensor_copy(ident[:], identf[:]).then_inc(consts_ready, 1)
            dve.tensor_scalar(rx[:], rx[:], 1.0 / VS, None, ALU.mult).then_inc(consts_ready, 1)
            dve.tensor_scalar(wa[:], wa[:], 1.0 / VS, None, ALU.mult).then_inc(consts_ready, 1)
            dve.tensor_scalar(wb[:], wb[:], 1.0 / VS, None, ALU.mult).then_inc(consts_ready, 1)
            dve.tensor_scalar(sel2[:], sel2[:], 1.0 / VS, None, ALU.mult).then_inc(consts_ready, 1)
            for i in range(2):
                dve.tensor_tensor(gb[:, i, D:3 * D], gb[:, i, D:3 * D], gb2[:, i, :], ALU.add
                                  ).then_inc(consts_ready, 1)
            dve.wait_ge(nall_ready, 1)
            nall_g = nall[:, 0:H].rearrange("p (g h) -> p g h", g=NG)
            dve.tensor_tensor(dd, s_neigh, nall_g.unsqueeze(2).to_broadcast([P, NG, T, GH]),
                              ALU.subtract).then_inc(dd_ready, 1)
            bn4 = bn[:].rearrange("p (c g) m h -> p g c m h", g=NG)
            ns4 = s_self.rearrange("p (c m) (g h) -> p g c m h", m=CT, g=NG)
            for g in range(NG):
                dve.tensor_tensor(bn4[:, g], ns4[:, g],
                                  nall_g[:, g].unsqueeze(1).unsqueeze(1).to_broadcast([P, NC, CT, GH]),
                                  ALU.add).then_inc(dve_step, k.up())
            dve.wait_ge(dve_step, k.now())
            dve.tensor_scalar(bn[:], bn[:], 0.0, None, ALU.max).then_inc(relu_ready, 1)
            dve.tensor_reduce(lmax[:, 0:1], nall[:], AX.X, ALU.max).then_inc(L_ready, 1)
            dve.wait_ge(L_ready, 1)
            dve.tensor_scalar(l16[:, 0:1], lmax[:, 0:1], 2.0 ** -20, 2.25, ALU.max, ALU.mult).then_inc(dve_step, k.up())
            dve.wait_ge(dve_step, k.now())
            dve.tensor_copy(lmax[:, 1:2], l16[:, 0:1]).then_inc(L_ready, 1)
            dve.wait_ge(L_ready, 2)
            dve.wait_ge(zeroed, 9)
            dve.tensor_scalar(diagL[:], identf[:], lmax[:, 1:2], None, ALU.mult).then_inc(L_ready, 1)
            dve.tensor_scalar(rowL[0:1, :], lmax[0:1, 1:2].to_broadcast([1, P]), -1.0, None, ALU.mult
                              ).then_inc(L_ready, 1)
            dve.wait_ge(ry_ready, 1)
            dve.tensor_scalar(ry[:].rearrange("p k w -> p (k w)"), ps[:, 0, 0:384], 1.0 / VS, None, ALU.mult
                              ).then_inc(consts_ready, 1)
            dve.wait_ge(exps_ready, 4)
            with dve.Fori(0, NB // 4) as b4:
                kb = Count(b4 * (4 * K_BLOCK) + k.n)
                for pair in range(2):
                    for i in range(2):
                        b = b4 * 4 + (pair * 2 + i)
                        v4 = v18[i].rearrange("p (g x w) -> p g x w", g=NG, w=2 * VC)
                        dve.wait_ge(cast_done, b4 * 12 + (pair * 6 + i + 5))
                        f4 = obuf[:].rearrange("p (b g x d) -> p b g x d", b=NB, g=NG, d=DH)[:, b]
                        for half, e in enumerate((fac0, fac1)):
                            eb = e.rearrange("p g (b t) h -> p b g (t h)", b=NB)[:, b].unsqueeze(3)
                            lo = half * VC
                            dve.tensor_tensor(v4[:, :, :, lo:lo + DH], f4,
                                              eb.to_broadcast([P, NG, BT * GH, DH]), ALU.mult
                                              ).then_inc(dve_step, kb.up())
                            last = dve.tensor_scalar(v4[:, :, :, lo + DH:lo + VC], eb, 1.0, None, ALU.mult)
                            if half == 0:
                                last.then_inc(dve_step, kb.up())
                        last.then_inc(rest_ready, 1)
                    for s in range(SPLIT - 1):
                        for i in range(2):
                            dve.wait_ge(dve_step, kb.now())
                            dve.wait_ge(rest_ready, b4 * 12 + (pair * 6 + s * 2 + i + 1))
                            dve.wait_ge(cast_done, b4 * 12 + (pair * 6 + s * 2 + i + 7))
                            v3 = v18[i].rearrange("p (x k) -> p x k", k=VC)
                            dve.tensor_tensor(v3, v3, wst_parts[pair * 2 + i][:, :, s * VC:(s + 1) * VC],
                                              ALU.subtract).then_inc(rest_ready, 1)
                assert kb.n == 4 * K_BLOCK, kb.n
            k.n += NB * K_BLOCK
            dve.wait_ge(hs_in, 32)
            dve.tensor_scalar(hparts[:, 0, :], identf[:], 0.0, 1.0, ALU.mult, ALU.add).then_inc(hs_split, 1)
            for s in range(SPLIT):
                dve.tensor_scalar(hparts[:, s + 1, :], hsrc, 1.0, None, ALU.mult).then_inc(hs_split, 1)
                if s < SPLIT - 1:
                    dve.wait_ge(hs_split, 2 * s + 2)
                    dve.tensor_tensor(hsrc, hsrc, hparts[:, s + 1, :], ALU.subtract).then_inc(hs_split, 1)
                    dve.wait_ge(hs_split, 2 * s + 3)
            for w in range(2):
                dve.wait_ge(w_stored[w], 16 + 4 * NB)

            def per_row(a, tiles=HT):
                return a.unsqueeze(2).to_broadcast([P, tiles, D])

            def post(it, g, kp):
                dve.wait_ge(z_ready, it + 2)
                dve.wait_ge(dve_step, kp.now())
                masked_sums = z0[:, :, 0:2 * GH * VC].rearrange("p m (h k) -> p m h k", h=GH)
                all_sums = z0[:, :, 2 * GH * VC:3 * GH * VC].rearrange("p m (h k) -> p m h k", h=GH)
                dve.tensor_copy(t1[:], all_sums).then_inc(dve_step, kp.up())
                dve.tensor_scalar(rdeg[:, it, :], z0[:, :, 3 * GH * VC], 1.0, None, ALU.add
                                  ).then_inc(dve_step, kp.up())
                dve.wait_ge(dve_step, kp.now())
                dve.tensor_tensor(t1[:], t1[:], masked_sums[:, :, :, VC:2 * VC], ALU.subtract
                                  ).then_inc(dve_step, kp.up())
                dve.wait_ge(dve_step, kp.now())
                dve.wait_ge(bn_ready, 1)
                dve.tensor_tensor(t1[:], t1[:], bn[:, it, :, :].unsqueeze(3).to_broadcast([P, CT, GH, VC]),
                                  ALU.mult).then_inc(dve_step, kp.up())
                dve.wait_ge(dve_step, kp.now())
                dve.tensor_tensor(t1[:], t1[:], masked_sums[:, :, :, 0:VC], ALU.add).then_inc(z_used, 1)
                dve.wait_ge(z_used, it + 2)
                dve.reciprocal(rden[:], t1[:, :, :, DH]).then_inc(dve_step, kp.up())
                dve.wait_ge(dve_step, kp.now())
                dve.tensor_tensor(o_now[:, g, :, :].rearrange("p m (h d) -> p m h d", h=GH),
                                  t1[:, :, :, 0:DH], rden[:].unsqueeze(3).to_broadcast([P, CT, GH, DH]),
                                  ALU.mult).then_inc(dve_step, kp.up())

            def norm_step(i, kk, u, q, st, tiles, dst):
                total, var, seed, half, y = (st[:, i, :] for i in range(5))
                dve.wait_ge(dve_step, kk.now())
                if i == 0:
                    op = dve.tensor_reduce(total, u, AX.X, ALU.add)
                elif i == 1:
                    op = dve.scalar_tensor_tensor(out=u, in0=per_row(total, tiles), scalar=-1.0 / D, in1=u,
                                                  op0=ALU.mult, op1=ALU.add)
                elif i == 2:
                    op = dve.tensor_tensor(q, u, u, ALU.mult)
                elif i == 3:
                    op = dve.tensor_reduce(var, q, AX.X, ALU.add)
                elif i == 4:
                    op = dve.tensor_scalar(var, var, 1.0 / D, EPS, ALU.mult, ALU.add)
                elif i == 5:
                    dve.tensor_scalar(half, var, -0.5, None, ALU.mult).then_inc(dve_step, kk.up())
                    op = dve.tensor_scalar(seed.bitcast(I32), var.bitcast(I32), 1, None,
                                           ALU.logical_shift_right)
                elif i == 6:
                    op = dve.tensor_scalar(y.bitcast(I32), seed.bitcast(I32), -1.0, float(0x5f3759df),
                                           ALU.mult, ALU.add)
                elif i == NORM_STEPS:
                    op = dve.tensor_tensor(dst, u, per_row(y, tiles), ALU.mult)
                elif i % 3 == 1:
                    op = dve.tensor_tensor(seed, y, y, ALU.mult)
                elif i % 3 == 2:
                    op = dve.tensor_tensor(seed, seed, half, ALU.mult)
                else:
                    op = dve.scalar_tensor_tensor(out=y, in0=seed, scalar=1.5, in1=y, op0=ALU.add, op1=ALU.mult)
                op.then_inc(dve_step, kk.up())

            def split_step(i, kk, src, dst):
                high, low = dst[:, :, 0:D], dst[:, :, D:2 * D]
                dve.wait_ge(dve_step, kk.now())
                if i == 0:
                    dve.tensor_scalar(high, src, VS, None, ALU.mult).then_inc(dve_step, kk.up())
                else:
                    dve.scalar_tensor_tensor(out=low, in0=src, scalar=VS, in1=high, op0=ALU.mult,
                                             op1=ALU.subtract).then_inc(v_ready, 1)

            def first_norm_step(i, c, kk):
                x_own = x_ch[:, c, :, :]
                if i == 0:
                    for g in range(NG):
                        dve.wait_ge(dve_step, kk.now())
                        dve.tensor_tensor(u_ch[:, :, g * 32:(g + 1) * 32], o_now[:, g, :, :],
                                          b0[:, g * 32:(g + 1) * 32].unsqueeze(1).to_broadcast([P, CT, 32]),
                                          ALU.add).then_inc(dve_step, kk.up())
                elif i == 1:
                    dve.wait_ge(dve_step, kk.now())
                    dve.wait_ge(x_in, 16)
                    dve.scalar_tensor_tensor(out=u_ch[:], in0=u_ch[:], scalar=0.0, in1=x_own, op0=ALU.max,
                                             op1=ALU.add).then_inc(dve_step, kk.up())
                elif i < 3 + NORM_STEPS:
                    norm_step(i - 2, kk, u_ch[:], q_ch[:], st_ch[:], CT, x_own)
                else:
                    split_step(i - 3 - NORM_STEPS, kk, x_own, vals_ch[:, c, :, :])

            def attention_step(c, g, kk, behind, norm_behind):
                it = c * NG + g
                for jt in range(T + 1):
                    if jt < T:
                        dve.wait_ge(tiles_done, it * T + slot_free(jt))
                        if jt == 0:
                            dve.wait_ge(s_loaded[g], c * 16 + 16)
                        for h in dve_heads(g, jt):
                            dve.tensor_scalar(masks[:, jt % RING, h, :, :].rearrange("p f k -> p (f k)"),
                                              srow[g][:, h, :], nthr[:, g, jt, h:h + 1], ONE8, ALU.is_gt,
                                              ALU.mult).then_inc(cmp_v, 1)
                    if jt > 0:
                        j = jt - 1
                        b, t = j // BT, j % BT
                        if t == 0:
                            dve.wait_ge(a_loaded[b], c * 16 + 16)
                        dve.wait_ge(cmp_v, cmp_v_at(c, g, j))
                        heads = GH - 1 if routed(j) else GH
                        dve.wait_ge(cmp_s, cmp_s_at(c, g, j, GH - heads))
                        m = masks16[:, j % RING, 0:heads, :, :]
                        dve.tensor_tensor(m, m, a16[:, b, :, t, :].unsqueeze(1).to_broadcast(
                            [P, heads, 2, HALF // 2]), ALU.bitwise_and).then_inc(masked, 1)
                    if behind and jt == 8:
                        post(it - 1, 1 - g, kk)
                    if norm_behind and jt >= 12 and (jt - 12) // 2 < 5 + NORM_STEPS and jt % 2 == 0:
                        first_norm_step((jt - 12) // 2, c - 1, kk)

            kk = Count(k.n)
            attention_step(0, 0, kk, False, False)
            attention_step(0, 1, kk, True, False)
            assert kk.now() == k.n + K_POST, kk.n
            k0 = kk.now()
            with dve.Fori(1, NC) as c:
                kk = Count((c - 1) * (2 * K_POST + K_FIRST) + k0)
                attention_step(c, 0, kk, True, True)
                attention_step(c, 1, kk, True, False)
                assert kk.n == 2 * K_POST + K_FIRST, kk.n
            kk = Count(k0 + (NC - 1) * (2 * K_POST + K_FIRST))
            post(IT - 1, 1, kk)
            for i in range(5 + NORM_STEPS):
                first_norm_step(i, NC - 1, kk)
            dve.wait_ge(cmp_s, NC * sum(S_CMP) + 1)
            dve.wait_ge(dve_step, kk.now())
            dve.reciprocal(rdeg[:], rdeg[:]).then_inc(dve_step, kk.up())
            k0 = kk.now()

            def norm(kk, dst):
                for i in range(NORM_STEPS + 1):
                    norm_step(i, kk, u, q, st, HT, dst)

            def split(kk, src, dst):
                for i in range(2):
                    split_step(i, kk, src, dst)

            def epilogue(p, c, f, k0):
                hf = c * 2 + f
                n = c * 2 + ((p - 1) * NH + f)
                kk = Count(c * (2 * K_PASS[p]) + (f * K_PASS[p] + k0))
                z = zz[f]
                if p < 4:
                    dve.wait_ge(v_ready, n + NC)
                else:
                    dve.wait_ge(row_out, c * 2 + (f + 1))
                dve.wait_ge(dve_step, kk.now())
                dve.wait_ge(zz_ready, n + 1)
                x_own = x_hf[:, hf, :, :]
                if p == 1:
                    dot = st[:, 5, :]
                    dve.tensor_tensor(q, z[:, :, 0:D], x_own, ALU.mult).then_inc(zz_used, 1)
                    dve.wait_ge(zz_used, n + 2)
                    dve.tensor_reduce(dot, q, AX.X, ALU.add).then_inc(dve_step, kk.up())
                    dve.scalar_tensor_tensor(out=u, in0=x_own, scalar=-0.1, in1=x_own, op0=ALU.mult, op1=ALU.add
                                             ).then_inc(dve_step, kk.up())
                    dve.wait_ge(dve_step, kk.now())
                    dve.tensor_scalar(dot, dot, -0.01, 1.0, ALU.mult, ALU.add).then_inc(dve_step, kk.up())
                    dve.wait_ge(dve_step, kk.now())
                    dve.tensor_tensor(u, u, per_row(dot), ALU.add).then_inc(dve_step, kk.up())
                    norm(kk, x_own)
                    split(kk, x_own, vals[1][:, hf, :, :])
                elif p < 4:
                    xin = x_own if p == 2 else h_hf[:, hf, :, :]
                    dve.tensor_tensor(gates, z, gb[:, p - 2, :].unsqueeze(1).to_broadcast([P, HT, GATES]),
                                      ALU.add).then_inc(zz_used, 1)
                    dve.wait_ge(gates_out, n - (NH - 1))
                    dve.tensor_tensor(nn[:], gates[:, :, D:2 * D], gates[:, :, 0:D], ALU.mult
                                      ).then_inc(dve_step, kk.up())
                    dve.wait_ge(dve_step, kk.now())
                    dve.tensor_tensor(nn[:], nn[:], gates[:, :, 3 * D:4 * D], ALU.add).then_inc(cand_in, 1)
                    dve.wait_ge(cand_out, n - (NH - 1))
                    dve.tensor_tensor(hh[:], xin, nn[:], ALU.subtract).then_inc(dve_step, kk.up())
                    dve.wait_ge(dve_step, kk.now())
                    dve.tensor_tensor(hh[:], hh[:], gates[:, :, 2 * D:3 * D], ALU.mult).then_inc(dve_step, kk.up())
                    dve.wait_ge(dve_step, kk.now())
                    dve.tensor_tensor(hh[:], hh[:], nn[:], ALU.add).then_inc(dve_step, kk.up())
                    dve.wait_ge(dve_step, kk.now())
                    if p == 2:
                        dve.tensor_scalar(h_hf[:, hf, :, :], hh[:], 0.0, None, ALU.max).then_inc(dve_step, kk.up())
                        split(kk, h_hf[:, hf, :, :], vals[0][:, hf, :, :])
                    else:
                        dve.scalar_tensor_tensor(out=u, in0=hh[:], scalar=0.0, in1=x_own, op0=ALU.max,
                                                 op1=ALU.add).then_inc(dve_step, kk.up())
                        norm(kk, x_own)
                        split(kk, x_own, vals[1][:, hf, :, :])
                else:
                    own = rdeg[:, c * 2, f * HT:(f + 1) * HT]
                    dve.tensor_tensor(u, z[:, :, D:2 * D], per_row(own), ALU.mult).then_inc(dve_step, kk.up())
                    dve.wait_ge(dve_step, kk.now())
                    dve.tensor_tensor(u, u, z[:, :, 0:D], ALU.add).then_inc(zz_used, 1)
                    dve.wait_ge(zz_used, n + 2)
                    dve.tensor_tensor(u, u, x_own, ALU.add).then_inc(dve_step, kk.up())
                    for i in range(NORM_STEPS):
                        norm_step(i, kk, u, q, st, HT, None)
                    dve.wait_ge(dve_step, kk.now())
                    dve.tensor_tensor(h_hf[:, hf, :, :], u, per_row(st[:, 4, :]), ALU.mult).then_inc(row_out, 1)
                assert kk.n == K_PASS[p], (p, kk.n)

            for p in range(1, 5):
                with dve.Fori(0, NC) as c:
                    for f in range(2):
                        epilogue(p, c, f, k0)
                k0 += NH * K_PASS[p]


_F32_INPUTS = ("adj", "xT", "xN", "W0", "attS", "attN", "bias0", "W1T", "wihT", "whhT", "bih", "bhh", "W3T",
               "consts")


def kernel(**inputs):
    import numpy as np
    import concourse.bacc as bacc
    from concourse.bass_utils import run_bass_kernel_spmd

    a = {k: np.asarray(v) for k, v in inputs.items()}

    add_pairs = np.zeros((P, 4 * VC), np.float32)
    add_all = np.zeros((P, GH * VC + 1), np.float32)
    for h in range(2):
        for s in range(SPLIT):
            for c in range(VC):
                e1_row, e2_row = (0, EW) if h == 0 else (HW + EW, HW)
                add_pairs[e1_row + s * VC + c, h * 2 * VC + c] = 1
                add_pairs[e2_row + s * VC + c, h * 2 * VC + VC + c] = 1
                for pair in range(2):
                    add_all[pair * HW + h * EW + s * VC + c, (pair * 2 + h) * VC + c] = 1
    add_all[ONES_AT - E2_AT, GH * VC] = 1
    eye = np.eye(P, dtype=np.float32)
    add_two = np.concatenate([eye[:D, :D], eye[:D, :D]])

    x, adj = a["x"], a["adj"]
    arrays = {
        "adj": np.ascontiguousarray(
            adj.reshape(NC, 2, HALF, NB, BT, P).transpose(0, 3, 5, 1, 4, 2)).reshape(NC, NB, P, -1),
        "xT": np.ascontiguousarray(x.T),
        "xN": np.ascontiguousarray(x.reshape(T, P, D).transpose(1, 0, 2)).reshape(P, T * D),
        "W0": a["L0_gnn_W"],
        "attS": a["L0_gnn_att_self"].reshape(D),
        "attN": a["L0_gnn_att_neigh"].reshape(D),
        "bias0": a["L0_gnn_bias"].reshape(D),
        "W1T": np.stack([a["L2_gnn_W1"].T, a["L2_gnn_W2"].T]),
        "wihT": np.stack([a["L2_gnn_wih1"].T, a["L2_gnn_wih2"].T]),
        "whhT": np.stack([a["L2_gnn_whh1"].T, a["L2_gnn_whh2"].T]),
        "bih": np.stack([a["L2_gnn_bih1"], a["L2_gnn_bih2"]]),
        "bhh": np.stack([a["L2_gnn_bhh1"], a["L2_gnn_bhh2"]]),
        "W3T": np.ascontiguousarray(a["L3_gnn_W"].T),
        "consts": np.concatenate([eye, add_pairs, add_all, add_two], axis=1),
    }
    nc = bacc.Bacc("TRN2", target_bir_lowering=False, num_devices=1)
    sent = {f"in_{k}": np.ascontiguousarray(arrays[k]) for k in _F32_INPUTS}
    aps = [nc.dram_tensor(k, v.shape, F32, kind="ExternalInput").ap() for k, v in sent.items()]
    out = nc.dram_tensor("out", (P, NH, HT * D), F32, kind="ExternalOutput").ap()
    build(nc, *aps, out)
    r = run_bass_kernel_spmd(nc, [sent], core_ids=[0])
    return np.ascontiguousarray(
        r.results[0]["out"].reshape(P, T, D).transpose(1, 0, 2)).reshape(N, D)
```
